# Optimizing a Trainium2 kernel written in Bass

```python
import numpy as np
import jax
import jax.numpy as jnp

def _softmax(x, axis=-1):
    return jax.nn.softmax(x, axis=axis)

def _gelu(x):
    return jax.nn.gelu(x, approximate=True)

def _silu(x):
    return jax.nn.silu(x)

def _sigmoid(x):
    return jax.nn.sigmoid(x)

def _layernorm(x, axis=-1, eps=1e-05):
    m = jnp.mean(x, axis=axis, keepdims=True)
    v = jnp.var(x, axis=axis, keepdims=True)
    return (x - m) / jnp.sqrt(v + eps)

def _scatter_add(tgt, idx, src, axis=0):
    return tgt.at[idx].add(src)

def _segment_sum(src, seg, n):
    return jax.ops.segment_sum(src, seg, n)
kernel_name = 'mk_xattn_ffn_d1_seqx_r2_882e9a'

def setup_inputs(seed: int=0):
    np.random.seed(seed)
    _w = jnp.asarray

    def _rec_inputs():
        import jax
        import jax.numpy as jnp
        _rk = jax.random.key(seed)
        x = -0.0002928 + 1 * jax.random.normal(jax.random.fold_in(_rk, 1), (4, 2048, 512), jnp.float32)
        _lenS = 2048 - jax.random.randint(jax.random.fold_in(_rk, 7), (4,), 0, max(1, 2048 // 4) + 1, jnp.int32)
        _lenS2 = 128 - jax.random.randint(jax.random.fold_in(_rk, 8), (4,), 0, max(1, 128 // 4) + 1, jnp.int32)
        _ctx_768P = jax.random.normal(jax.random.fold_in(_rk, 11), (4, 16, 384), jnp.float32)
        _ctx_768c = jax.random.dirichlet(jax.random.fold_in(_rk, 511), 0.3 * jnp.ones((16,), jnp.float32), (4, 128))
        _ctx_768t = jnp.einsum('bsk,bkd->bsd', _ctx_768c, _ctx_768P)
        _ctx_768t = _ctx_768t * jax.lax.rsqrt(jnp.mean(jnp.square(_ctx_768t)) + 1e-12) * 0.953939
        ctx_768 = 2.09791e-05 + 1.00001 * (_ctx_768t + 0.3 * jax.random.normal(jax.random.fold_in(_rk, 611), (4, 128, 384), jnp.float32))
        return (x, ctx_768)
    x, ctx_768 = _rec_inputs()

    def _L0_xattn_setup():
        import jax, jax.numpy as jnp
        import numpy as np
        N_HEADS = 16
        DIMS = 512
        D_CTX = 384
        HEAD = DIMS // N_HEADS
        key = jax.random.key(seed)
        ks = jax.random.split(key, 10)
        s_q = 1.0 / np.sqrt(DIMS)
        s_c = 1.0 / np.sqrt(D_CTX)
        return {'x': jax.random.normal(ks[0], (2, 1024, DIMS), jnp.float32), 'context': jax.random.normal(ks[1], (2, 1024, D_CTX), jnp.float32), 'w_q': jax.random.normal(ks[2], (DIMS, DIMS), jnp.float32) * s_q, 'b_q': jax.random.normal(ks[3], (DIMS,), jnp.float32) * 0.01, 'w_k': jax.random.normal(ks[4], (D_CTX, DIMS), jnp.float32) * s_c, 'b_k': jax.random.normal(ks[5], (DIMS,), jnp.float32) * 0.01, 'w_v': jax.random.normal(ks[6], (D_CTX, DIMS), jnp.float32) * s_c, 'b_v': jax.random.normal(ks[7], (DIMS,), jnp.float32) * 0.01, 'w_o': jax.random.normal(ks[8], (DIMS, DIMS), jnp.float32) * s_q, 'b_o': jax.random.normal(ks[9], (DIMS,), jnp.float32) * 0.01}
    _L0_xattn_all = _L0_xattn_setup()
    _L0_xattn_in = {k: v for k, v in _L0_xattn_all.items() if k in ('w_q', 'b_q', 'w_k', 'b_k', 'w_v', 'b_v', 'w_o', 'b_o')}
    del _L0_xattn_all

    def _L0_ffn_setup():
        import jax, jax.numpy as jnp
        import numpy as np
        INPUT_SIZE = 512
        OUTPUT_SIZE = 512
        key = jax.random.key(seed)
        kx, kt, kp, ktn, kpn = jax.random.split(key, 5)
        x = jax.random.normal(kx, (8, 1024, INPUT_SIZE), dtype=jnp.float32)
        theta = jax.random.normal(kt, (INPUT_SIZE, OUTPUT_SIZE), dtype=jnp.float32) * 0.02
        phi = jax.random.normal(kp, (INPUT_SIZE, OUTPUT_SIZE), dtype=jnp.float32) * 0.02
        theta_noise = jax.random.normal(ktn, (INPUT_SIZE, OUTPUT_SIZE), dtype=jnp.float32) * 0.01
        phi_noise = jax.random.normal(kpn, (INPUT_SIZE, OUTPUT_SIZE), dtype=jnp.float32) * 0.01
        return {'x': x, 'theta': theta, 'phi': phi, 'theta_noise': theta_noise, 'phi_noise': phi_noise}
    _L0_ffn_all = _L0_ffn_setup()
    _L0_ffn_in = {k: v for k, v in _L0_ffn_all.items() if k in ('theta', 'phi', 'theta_noise', 'phi_noise')}
    del _L0_ffn_all
    return {'x': x, 'ctx_768': ctx_768, 'L0_xattn_w_q': _L0_xattn_in['w_q'], 'L0_xattn_b_q': _L0_xattn_in['b_q'], 'L0_xattn_w_k': _L0_xattn_in['w_k'], 'L0_xattn_b_k': _L0_xattn_in['b_k'], 'L0_xattn_w_v': _L0_xattn_in['w_v'], 'L0_xattn_b_v': _L0_xattn_in['b_v'], 'L0_xattn_w_o': _L0_xattn_in['w_o'], 'L0_xattn_b_o': _L0_xattn_in['b_o'], 'L0_ffn_theta': _L0_ffn_in['theta'], 'L0_ffn_phi': _L0_ffn_in['phi'], 'L0_ffn_theta_noise': _L0_ffn_in['theta_noise'], 'L0_ffn_phi_noise': _L0_ffn_in['phi_noise']}

def reference(x, ctx_768, L0_xattn_w_q, L0_xattn_b_q, L0_xattn_w_k, L0_xattn_b_k, L0_xattn_w_v, L0_xattn_b_v, L0_xattn_w_o, L0_xattn_b_o, L0_ffn_theta, L0_ffn_phi, L0_ffn_theta_noise, L0_ffn_phi_noise):
    import jax
    import jax.numpy as jnp

    def _L0_xattn_ref(x, context, w_q, b_q, w_k, b_k, w_v, b_v, w_o, b_o):
        import jax, jax.numpy as jnp
        import numpy as np
        N_HEADS = 16
        DIMS = 512
        D_CTX = 384
        HEAD = DIMS // N_HEADS
        B, Lq, D = x.shape
        q = x @ w_q + b_q
        k = context @ w_k + b_k
        v = context @ w_v + b_v
        q = q.reshape(B, Lq, N_HEADS, HEAD)
        k = k.reshape(B, -1, N_HEADS, HEAD)
        v = v.reshape(B, -1, N_HEADS, HEAD)
        scale = 1.0 / np.sqrt(HEAD).astype(np.float32)
        scores = jnp.einsum('bqhd,bkhd->bhqk', q, k) * scale
        weights = jax.nn.softmax(scores, axis=-1)
        out = jnp.einsum('bhqk,bkhd->bqhd', weights, v).reshape(B, Lq, D)
        return out @ w_o + b_o

    def _L0_ffn_ref(x, theta, phi, theta_noise, phi_noise):
        import jax, jax.numpy as jnp
        import numpy as np
        INPUT_SIZE = 512
        OUTPUT_SIZE = 512
        real = jnp.einsum('bti,io->bto', x, jnp.cos(theta + theta_noise))
        imag = jnp.einsum('bti,io->bto', x, jnp.sin(phi + phi_noise))
        return jnp.sqrt(real * real + imag * imag)
    x = x + _L0_xattn_ref(_layernorm(x, axis=-1), ctx_768, L0_xattn_w_q, L0_xattn_b_q, L0_xattn_w_k, L0_xattn_b_k, L0_xattn_w_v, L0_xattn_b_v, L0_xattn_w_o, L0_xattn_b_o)
    x = x + _L0_ffn_ref(_layernorm(x, axis=-1), L0_ffn_theta, L0_ffn_phi, L0_ffn_theta_noise, L0_ffn_phi_noise)
    return x

_drawn_inputs = setup_inputs


def setup_inputs(seed=0):
    import zlib

    import numpy as np

    out = dict(_drawn_inputs(seed))
    spreads = {}
    factors = {'L0_xattn_b_q': 36.444,
     'L0_xattn_b_k': 64.0,
     'L0_xattn_b_v': 6.792,
     'L0_xattn_b_o': 6.531,
     'L0_ffn_theta': 8.0,
     'L0_ffn_theta_noise': 8.0}
    for name, (base, spread) in spreads.items():
        noise = np.random.default_rng([zlib.crc32(name.encode()), seed]).standard_normal(out[name].shape)
        drawn = base * np.exp(spread * noise) if base else spread * noise
        out[name] = jnp.asarray(drawn.astype(out[name].dtype))
    for name, factor in factors.items():
        out[name] = (out[name] * factor).astype(out[name].dtype)
    return out
```

```python
from contextlib import ExitStack

import concourse.bass as bass
from concourse import mybir

ALU = mybir.AluOpType
ACT = mybir.ActivationFunctionType
AX = mybir.AxisListType
F32 = mybir.dt.float32
F32R = mybir.dt.float32r

P = 128
NB = 4
LQ = 2048
LK = 128
D = 512
DC = 384
NH = 16
HD = D // NH
T = 256
SUB = T // P
NT = NB * LQ // T
FT = D // P
CT = DC // P
HG = P // HD
NG = NH // HG
PAIRS = NH // 2
SCALE = float(HD) ** -0.5
LN_EPS = 1e-5
KROWS = 3 * HD + 1
MAXROW = 3 * HD

PI = 3.14159265358979
TWO_PI_HI = 6.28125
TWO_PI_MID = 0.0019350051879882812
TWO_PI_LO = 2 * PI - TWO_PI_HI - TWO_PI_MID
ROUND = 1.5 * 2.0 ** 23
SIN_MAX = 3.1415925

CONSTS = 5
ANGLE_STEPS = 8

FIRST = -2
LOOP_FIRST = 1
LOOP_TURNS = 7
LAST = NT


class Tile:

    def __init__(self, turn, c):
        self.turn, self.c = turn, c
        self.static = isinstance(turn, int)

    def __add__(self, n):
        return Tile(self.turn, self.c + n)

    @property
    def exists(self):
        return not self.static or 0 <= self.c < NT

    @property
    def batch(self):
        return self.c % NB

    @property
    def chunk(self):
        return self.turn + self.c // NB

    def count(self, per, n):
        return self.turn * (NB * per) + (self.c * per + n)


def wait(eng, sem, tile, per, n):
    if not tile.static:
        eng.wait_ge(sem, tile.count(per, n))
    elif tile.c * per + n > 0:
        eng.wait_ge(sem, min(tile.c * per + n, NT * per))


def steps(eng, step):
    for c in range(FIRST, LOOP_FIRST):
        step(Tile(0, c))
    with eng.Fori(0, LOOP_TURNS) as turn:
        for c in range(LOOP_FIRST, LOOP_FIRST + NB):
            step(Tile(turn, c))
    for c in range(LOOP_FIRST + NB * LOOP_TURNS, LAST + 1):
        step(Tile(0, c))



def xattn_ffn(nc, x, ctx_768, w_q, b_q, w_k, b_k, w_v, b_v, w_o, b_o, theta, phi, theta_noise, phi_noise, out):
    with ExitStack() as stack:
        def sb(name, shape, dt=F32):
            return stack.enter_context(nc.sbuf_tensor(name, shape, dt))

        def ps(name, shape):
            return stack.enter_context(nc.psum_tensor(name, shape, F32))

        def sem(name):
            return stack.enter_context(nc.semaphore(name))

        ident = sb("ident", [P, P])
        ones = sb("ones", [P, HD])
        wq = sb("wq", [P, 2, FT, D], F32R)
        wo = sb("wo", [P, 2, FT, D], F32R)
        wcos = sb("wcos", [P, 2, FT, D], F32R)
        wsin = sb("wsin", [P, 2, FT, D], F32R)
        kstack = sb("kstack", [P, HG, NG, NB, LK], F32R)
        v_sb = sb("v_sb", [P, NB, D])
        bq_col = sb("bq_col", [P, FT])
        bk_col = sb("bk_col", [P, FT])
        bo_row = sb("bo_row", [P, D])
        minus_half = sb("minus_half", [P, 2 * SUB])

        kmask = sb("kmask", [P, NG, HG, LK], F32R)
        xres = sb("xres", [P, NB, SUB, D])
        xn = sb("xn", [P, 2, SUB, D])
        xt1 = sb("xt1", [P, 2, FT, T], F32R)
        xt2 = sb("xt2", [P, 2, FT, T], F32R)
        qt = sb("qt", [P, 2, NG, T], F32R)
        qstack = sb("qstack", [P, HG, NG, T], F32R)
        probs = sb("probs", [P, 4, 2, T])
        rden = sb("rden", [P, T])
        att = sb("att", [P, T])
        att_t = sb("att_t", [P, 2, FT, T], F32R)
        sq_real = sb("sq_real", [P, SUB, D])
        sq_imag = sb("sq_imag", [P, D])
        stats = sb("stats", [P, 2 * SUB, 6])
        meanvar = sb("meanvar", [P, 2 * SUB, 2])
        vareps = sb("vareps", [P, 2 * SUB])
        rstd = sb("rstd", [P, 2 * SUB])
        rowmax = sb("rowmax", [P, SUB, NH])
        negmax = sb("negmax", [NH, T], F32R)

        ctx_in = probs[:].rearrange("p a b n -> p (a b n)")[:, 0:NB * DC].rearrange("p (b c) -> p b c", b=NB)
        ctx_t = xn[:].rearrange("p a s d -> p (a s) d")[:, 0:CT, :]
        bv_row = sq_imag
        raw = [xres[:, 2 * i:2 * i + 2].rearrange("p b s d -> p (b s) d") for i in range(2)]
        raw += [probs[:].rearrange("p a b n -> p (a b n)").rearrange("p (f d) -> p f d", f=FT),
                xn[:].rearrange("p a s d -> p (a s) d")]
        kt_hi = xt1[:].rearrange("p a f t -> p (a f t)").rearrange("p (g b k) -> p g b k", g=NG, b=NB)
        kt_lo = xt2[:].rearrange("p a f t -> p (a f t)").rearrange("p (g b k) -> p g b k", g=NG, b=NB)

        gen = ps("gen", [P, 4, 512])
        scores = ps("scores", [P, 2, 2, T])
        values_sums = ps("values_sums", [P, 2, 2, T])

        consts_made = sem("consts_made")
        passed = sem("passed")
        ident_zero = sem("ident_zero")
        ctx_loaded = sem("ctx_loaded")
        wk_loaded = sem("wk_loaded")
        wv_loaded = sem("wv_loaded")
        bias_loaded = sem("bias_loaded")
        raw_loaded = [sem(f"raw{i}_loaded") for i in range(4)]
        ctxt_mm = sem("ctxt_mm")
        ctxt_ready = sem("ctxt_ready")
        kt_mm = sem("kt_mm")
        kthi_ready = sem("kthi_ready")
        ktlo_ready = sem("ktlo_ready")
        v_mm = sem("v_mm")
        v_ready = sem("v_ready")
        kstack_loaded = sem("kstack_loaded")
        whi_ready = sem("whi_ready")
        wlo_ready = sem("wlo_ready")
        angle_step = sem("angle_step")
        trig_ready = sem("trig_ready")
        x_loaded = [sem(f"x_loaded{b}") for b in range(NB)]
        out_stored = [sem(f"out_stored{b}") for b in range(NB)]
        bn_done = sem("bn_done")
        bn2_done = sem("bn2_done")
        stats_ready = sem("stats_ready")
        vareps_ready = sem("vareps_ready")
        rstd_ready = sem("rstd_ready")
        xn1_ready = sem("xn1_ready")
        xn2_ready = sem("xn2_ready")
        xb_ready = sem("xb_ready")
        tr1_mm = sem("tr1_mm")
        xt1_hi = sem("xt1_hi")
        xt1_ready = sem("xt1_ready")
        q_mm = sem("q_mm")
        q_hi = sem("q_hi")
        q_ready = sem("q_ready")
        qstack_loaded = sem("qstack_loaded")
        kmask_ready = sem("kmask_ready")
        smax_mm = sem("smax_mm")
        max_ready = sem("max_ready")
        maxt_mm = sem("maxt_mm")
        negmax_ready = sem("negmax_ready")
        negmax_loaded = sem("negmax_loaded")
        st_mm = sem("st_mm")
        exp_done = sem("exp_done")
        pv_mm = sem("pv_mm")
        rden_ready = sem("rden_ready")
        att_done = sem("att_done")
        att_hi = sem("att_hi")
        att_ready = sem("att_ready")
        wo_mm = sem("wo_mm")
        x2_ready = sem("x2_ready")
        tr2_mm = sem("tr2_mm")
        xt2_hi = sem("xt2_hi")
        xt2_ready = sem("xt2_ready")
        ffn_mm = sem("ffn_mm")
        sq_done = sem("sq_done")
        sum_ready = sem("sum_ready")
        root_ready = sem("root_ready")
        result_ready = sem("result_ready")

        x_tiles = x.rearrange("b (i p s) f -> b i p s f", p=P, s=SUB)
        out_tiles = out.rearrange("b (i p s) f -> b i p s f", p=P, s=SUB)

        def rows(w):
            return w.rearrange("(f p) n -> p f n", p=P)

        block = stack.enter_context(nc.Block())

        @block.sync
        def _(sp):
            sp.dma_start(ctx_in, ctx_768.rearrange("b p c -> p b c")).then_inc(ctx_loaded, 16)
            sp.dma_start(raw[0][:, 0:CT, :], rows(w_k)).then_inc(wk_loaded, 16)
            sp.dma_start(raw[1][:, 0:CT, :], rows(w_v)).then_inc(wv_loaded, 16)
            sp.dma_start(bq_col[:], b_q.rearrange("(f p) -> p f", p=P), allow_slow_non_contiguous=True).then_inc(bias_loaded, 16)
            sp.dma_start(bk_col[:], b_k.rearrange("(f p) -> p f", p=P), allow_slow_non_contiguous=True).then_inc(bias_loaded, 16)
            sp.dma_start(bv_row[:], b_v.partition_broadcast(P)).then_inc(bias_loaded, 16)
            sp.dma_start(bo_row[:], b_o.partition_broadcast(P)).then_inc(bias_loaded, 16)
            sp.wait_ge(ctxt_mm, CT)
            sp.dma_start(raw[2], rows(w_q)).then_inc(raw_loaded[2], 16)
            sp.wait_ge(kt_mm, NG)
            sp.dma_start(raw[0], rows(theta)).then_inc(raw_loaded[0], 16)
            sp.wait_ge(v_mm, NB)
            sp.dma_start(raw[1], rows(theta_noise)).then_inc(raw_loaded[1], 16)
            sp.dma_start(raw[3], rows(w_o)).then_inc(raw_loaded[3], 16)
            sp.wait_ge(kthi_ready, NG)
            sp.wait_ge(ktlo_ready, NG)
            for j in range(HG):
                for i, part in enumerate((kt_hi, kt_hi, kt_lo)):
                    sp.dma_start(kstack[HD * i:HD * (i + 1), j].bitcast(F32),
                                 part[HD * j:HD * (j + 1)].bitcast(F32)).then_inc(kstack_loaded, 16)
            sp.wait_ge(wlo_ready, 2)
            sp.dma_start(raw[2], rows(phi)).then_inc(raw_loaded[2], 16)
            sp.dma_start(raw[3], rows(phi_noise)).then_inc(raw_loaded[3], 16)
            sp.wait_ge(wlo_ready, 3)
            sp.dma_start(xres[:, 0], x_tiles[0, 0]).then_inc(x_loaded[0], 16)

            def step(s):
                new, done, load = s + 1, s + -1, s + 3
                if new.exists:
                    wait(sp, q_ready, new, 2, 2)
                    sp.sem_inc(passed, 1)
                    wait(sp, st_mm, s, PAIRS, PAIRS)
                    for j in range(HG):
                        for i, part in enumerate((0, 1, 0)):
                            sp.dma_start(qstack[HD * i:HD * (i + 1), j].bitcast(F32),
                                         qt[HD * j:HD * (j + 1), part].bitcast(F32)).then_inc(qstack_loaded, 16)
                    wait(sp, negmax_ready, new, 1, 1)
                    sp.dma_start(qstack[MAXROW:MAXROW + 1].rearrange("p j g t -> p (j g) t").bitcast(F32),
                                 negmax[:].bitcast(F32)).then_inc(negmax_loaded, 16)
                if done.exists:
                    wait(sp, result_ready, done, SUB, SUB)
                    sp.sem_inc(passed, 1)
                    sp.dma_start(out_tiles[done.batch, done.chunk], xres[:, done.batch]).then_inc(out_stored[done.batch], 16)
                if load.exists:
                    if done.exists:
                        sp.wait_ge(out_stored[done.batch], 16 * (done.chunk + 1))
                        sp.sem_inc(passed, 1)
                    sp.dma_start(xres[:, load.batch], x_tiles[load.batch, load.chunk]).then_inc(x_loaded[load.batch], 16)

            steps(sp, step)
            for b in range(NB):
                sp.wait_ge(out_stored[b], 16 * NT // NB)

        @block.gpsimd
        def _(pool):
            pool.memset(ident[:], 0.0).then_inc(ident_zero, 1)
            pool.wait_ge(ident_zero, 1)
            pool.affine_select(out=ident[:], in_=ident[:], compare_op=ALU.not_equal, fill=1.0, base=0,
                               pattern=[[-1, P]], channel_multiplier=1).then_inc(consts_made, 1)
            pool.memset(ones[:], 1.0).then_inc(consts_made, 1)
            pool.memset(minus_half[:], -0.5).then_inc(consts_made, 1)
            pool.wait_ge(consts_made, 3)
            pool.memset(kstack[MAXROW:MAXROW + 1].bitcast(F32), 1.0).then_inc(consts_made, 1)
            pool.wait_ge(consts_made, 4)
            pool.memset(kmask[:].bitcast(F32), 0.0).then_inc(consts_made, 1)
            pool.wait_ge(consts_made, CONSTS)
            pool.wait_ge(bias_loaded, 64)

            def step(s):
                new, done = s + 2, s + -1
                lo, hi = 0 if new.exists else SUB, 2 * SUB if s.exists else SUB
                if new.exists or s.exists:
                    pool.wait_ge(stats_ready, new.count(1, 1))
                    wait(pool, xn1_ready, new, 1, 0)
                    wait(pool, xn2_ready, done, 1, 1)
                    pool.sem_inc(passed, 1)
                    pool.tensor_scalar(vareps[:, lo:hi], meanvar[:, lo:hi, 1], LN_EPS, None, ALU.add).then_inc(vareps_ready, 1)
                    pool.wait_ge(vareps_ready, new.count(1, 1))
                    pool.tensor_tensor(rstd[:, lo:hi], vareps[:, lo:hi], minus_half[:, lo:hi], ALU.pow).then_inc(rstd_ready, 1)
                if new.exists:
                    wait(pool, xn1_ready, new, 1, 1)
                    for w in range(SUB):
                        last = pool.tensor_tensor(xres[:, new.batch, w], xres[:, new.batch, w], bo_row[:], ALU.add)
                    last.then_inc(xb_ready, 1)
                if done.exists:
                    wait(pool, root_ready, done, 1, 1)
                    for w in range(SUB):
                        pool.tensor_tensor(xres[:, done.batch, w], xres[:, done.batch, w], sq_real[:, w],
                                           ALU.add).then_inc(result_ready, 1)

            steps(pool, step)

        @block.scalar
        def _(act):
            for c in range(CT):
                act.wait_ge(ctxt_mm, c + 1)
                act.activation(ctx_t[:, c, :], gen[:, c, :], ACT.Copy).then_inc(ctxt_ready, 1)
            act.wait_ge(bias_loaded, 64)
            for g in range(NG):
                act.wait_ge(kt_mm, g + 1)
                act.activation(kt_hi[:, g].rearrange("p b k -> p (b k)"), gen[:, g, :], ACT.Identity,
                               bias=bk_col[:, g:g + 1]).then_inc(kthi_ready, 1)
            for i, (src, w) in enumerate(((2, wq), (3, wo))):
                act.wait_ge(raw_loaded[src], 16)
                act.activation(w[:, 0], raw[src], ACT.Copy).then_inc(whi_ready, 1)
            for i, (src, w) in enumerate(((0, wcos), (2, wsin))):
                act.wait_ge(angle_step, ANGLE_STEPS * (i + 1))
                act.activation(raw[src], raw[src], ACT.Sin).then_inc(trig_ready, 1)
                act.wait_ge(trig_ready, i + 1)
                act.activation(w[:, 0], raw[src], ACT.Copy).then_inc(whi_ready, 1)
            act.wait_ge(kstack_loaded, 16 * 3 * HG)
            act.wait_ge(consts_made, CONSTS)

            def step(s):
                q_tile, t1, ffn = s + 1, s + 2, s + -1
                if s.exists:
                    for k in range(PAIRS):
                        wait(act, st_mm, s, PAIRS, k + 1)
                        wait(act, pv_mm, s, NG, k // 2 - 1)
                        act.activation(probs[:, k % 4], scores[:, k % 2], ACT.Exp, scale=SCALE).then_inc(exp_done, 1)
                if q_tile.exists:
                    wait(act, qstack_loaded, s, 16 * 3 * HG, 16 * 3 * HG)
                    wait(act, smax_mm, s, SUB * NG, SUB * NG)
                    for k in range(2):
                        wait(act, q_mm, q_tile, 2, k + 1)
                        for i in range(2):
                            g = 2 * k + i
                            last = act.activation(qt[:, 0, g], gen[:, 1 + k, T * i:T * (i + 1)], ACT.Identity,
                                                  bias=bq_col[:, g:g + 1])
                        last.then_inc(q_hi, 1)

                def square(u):
                    wait(act, ffn_mm, ffn, 2 * SUB, u + 1)
                    if u == 0:
                        wait(act, result_ready, ffn, SUB, 0)
                    if u % 2:
                        wait(act, sum_ready, ffn, SUB, u // 2)
                    act.activation(sq_imag[:] if u % 2 else sq_real[:, u // 2], gen[:, (1, 2, 3, 3)[u], :],
                                   ACT.Square).then_inc(sq_done, 1)

                if ffn.exists:
                    for u in range(3):
                        square(u)
                if t1.exists:
                    wait(act, smax_mm, q_tile, SUB * NG, SUB * NG)
                    for j in range(HG):
                        last = act.activation(kmask[HD * j:HD * (j + 1), :, j, :],
                                              kstack[0:HD, j, :, t1.batch, :].bitcast(F32), ACT.Copy)
                    last.then_inc(kmask_ready, 1)
                    wait(act, q_mm, q_tile, 2, 2)
                    for k in range(2):
                        wait(act, tr1_mm, t1, 2, k + 1)
                        act.activation(xt1[:, 0, 2 * k:2 * k + 2].rearrange("p f t -> p (f t)"), gen[:, k, :],
                                       ACT.Copy).then_inc(xt1_hi, 1)
                if q_tile.exists:
                    wait(act, maxt_mm, q_tile, 1, 1)
                    wait(act, negmax_loaded, s, 16, 16)
                    act.activation(negmax[:], gen[0:NH, 2, 0:T], ACT.Copy, scale=-1.0).then_inc(negmax_ready, 1)
                if ffn.exists:
                    square(3)
                if s.exists:
                    wait(act, ffn_mm, ffn, 2 * SUB, 2 * SUB)
                    for k in range(2):
                        wait(act, tr2_mm, s, 2, k + 1)
                        act.activation(xt2[:, 0, 2 * k:2 * k + 2].rearrange("p f t -> p (f t)"), gen[:, k, :],
                                       ACT.Copy).then_inc(xt2_hi, 1)
                if ffn.exists:
                    wait(act, sum_ready, ffn, SUB, SUB)
                    act.activation(sq_real[:], sq_real[:], ACT.Sqrt).then_inc(root_ready, 1)

            steps(act, step)

        @block.vector
        def _(dve):
            dve.wait_ge(bias_loaded, 64)
            for g in range(NG):
                dve.wait_ge(kthi_ready, g + 1)
                dve.scalar_tensor_tensor(kt_lo[:, g].rearrange("p b k -> p (b k)"), gen[:, g, :], bk_col[:, g:g + 1],
                                         kt_hi[:, g].rearrange("p b k -> p (b k)").bitcast(F32),
                                         ALU.add, ALU.subtract).then_inc(ktlo_ready, 1)
            for b in range(NB):
                dve.wait_ge(v_mm, b + 1)
                dve.tensor_tensor(v_sb[:, b], gen[:, b, :], bv_row[:], ALU.add).then_inc(v_ready, 1)
            for i, (src, w) in enumerate(((2, wq), (3, wo))):
                dve.wait_ge(whi_ready, i + 1)
                dve.tensor_tensor(w[:, 1], raw[src], w[:, 0].bitcast(F32), ALU.subtract).then_inc(wlo_ready, 1)
            for i, (a, b, offset, w) in enumerate(((0, 1, PI / 2, wcos), (2, 3, 0.0, wsin))):
                y, k = raw[a], raw[b]
                n = ANGLE_STEPS * i
                dve.wait_ge(raw_loaded[a], 16 if a < 2 else 32)
                dve.wait_ge(raw_loaded[b], 16 if b < 2 else 32)
                dve.tensor_tensor(y, y, k, ALU.add).then_inc(angle_step, 1)
                dve.wait_ge(angle_step, n + 1)
                dve.tensor_scalar(k, y, 1.0 / (2 * PI), offset / (2 * PI), ALU.mult, ALU.add).then_inc(angle_step, 1)
                dve.wait_ge(angle_step, n + 2)
                dve.tensor_scalar(k, k, ROUND, ROUND, ALU.add, ALU.subtract).then_inc(angle_step, 1)
                for m, part in enumerate((TWO_PI_HI, TWO_PI_MID, TWO_PI_LO)):
                    dve.wait_ge(angle_step, n + 3 + m)
                    dve.scalar_tensor_tensor(y, k, -part, y, ALU.mult, ALU.add).then_inc(angle_step, 1)
                dve.wait_ge(angle_step, n + 6)
                dve.tensor_scalar(y, y, offset, SIN_MAX, ALU.add, ALU.min).then_inc(angle_step, 1)
                dve.wait_ge(angle_step, n + 7)
                dve.tensor_scalar(y, y, -SIN_MAX, None, ALU.max).then_inc(angle_step, 1)
                dve.wait_ge(whi_ready, 3 + i)
                dve.tensor_tensor(w[:, 1], raw[a], w[:, 0].bitcast(F32), ALU.subtract).then_inc(wlo_ready, 1)

            def step(s):
                q_tile, t1, ffn = s + 1, s + 2, s + -1
                if s.exists:
                    wait(dve, wo_mm, s, SUB, 0)
                    for g in range(NG):
                        wait(dve, pv_mm, s, NG, g + 1)
                        wait(dve, att_done, s, NG, g)
                        dve.reciprocal(rden[:], values_sums[:, g % 2, 1]).then_inc(rden_ready, 1)
                        wait(dve, rden_ready, s, NG, g + 1)
                        wait(dve, att_ready, s, NG, g)
                        dve.tensor_tensor(att[:], values_sums[:, g % 2, 0], rden[:], ALU.mult).then_inc(att_done, 1)
                        wait(dve, att_done, s, NG, g + 1)
                        dve.tensor_copy(att_t[:, 0, g], att[:]).then_inc(att_hi, 1)
                        wait(dve, att_hi, s, NG, g + 1)
                        dve.tensor_tensor(att_t[:, 1, g], att[:], att_t[:, 0, g].bitcast(F32),
                                          ALU.subtract).then_inc(att_ready, 1)
                if q_tile.exists:
                    for k in range(2):
                        wait(dve, q_hi, q_tile, 2, k + 1)
                        for i in range(2):
                            g = 2 * k + i
                            last = dve.scalar_tensor_tensor(qt[:, 1, g], gen[:, 1 + k, T * i:T * (i + 1)],
                                                            bq_col[:, g:g + 1], qt[:, 0, g].bitcast(F32),
                                                            ALU.add, ALU.subtract)
                        last.then_inc(q_ready, 1)
                if s.exists:
                    wait(dve, xb_ready, s, 1, 1)
                    for w in range(SUB):
                        wait(dve, wo_mm, s, SUB, w + 1)
                        dve.tensor_tensor(xres[:, s.batch, w], gen[:, (3, 0)[w], :], xres[:, s.batch, w],
                                          ALU.add).then_inc(x2_ready, 1)
                        wait(dve, x2_ready, s, SUB, w + 1)
                        dve.bn_stats(stats[:, SUB + w], xres[:, s.batch, w]).then_inc(bn2_done, 1)
                if t1.exists:
                    dve.wait_ge(x_loaded[t1.batch], 16 * (t1.chunk + 1))
                    for w in range(SUB):
                        dve.bn_stats(stats[:, w], xres[:, t1.batch, w]).then_inc(bn_done, 1)
                    wait(dve, bn_done, t1, SUB, SUB)
                    dve.sem_inc(passed, 1)
                    for w in range(SUB):
                        last = dve.bn_aggr(meanvar[:, w], stats[:, w])
                if s.exists:
                    wait(dve, bn2_done, s, SUB, SUB)
                    dve.sem_inc(passed, 1)
                    for w in range(SUB, 2 * SUB):
                        last = dve.bn_aggr(meanvar[:, w], stats[:, w])
                if t1.exists or s.exists:
                    last.then_inc(stats_ready, 1)
                if q_tile.exists:
                    wait(dve, maxt_mm, s, 1, 1)
                    for i in range(SUB * NG):
                        w, g = i // NG, i % NG
                        wait(dve, smax_mm, q_tile, SUB * NG, i + 1)
                        dve.tensor_reduce(rowmax[:, w].rearrange("p (j g) -> p g j", g=NG)[:, g],
                                          gen[:, (1, 2, 3, 0)[i % 4], :].rearrange("p (j k) -> p j k", j=HG),
                                          AX.X, ALU.max).then_inc(max_ready, 1)
                for tile, part, transposed, ready in ((s, 1, tr2_mm, xn2_ready), (t1, 0, tr1_mm, xn1_ready)):
                    if tile.exists:
                        dve.wait_ge(rstd_ready, t1.count(1, 1))
                        dve.wait_ge(stats_ready, t1.count(1, 1))
                        wait(dve, transposed, tile, 2, 0)
                        for w in range(SUB):
                            r = SUB * part + w
                            last = dve.tensor_scalar(xn[:, part, w], xres[:, tile.batch, w], meanvar[:, r, 0:1],
                                                     rstd[:, r:r + 1], ALU.subtract, ALU.mult)
                        last.then_inc(ready, 1)

                def add_squares(w):
                    wait(dve, sq_done, ffn, 2 * SUB, 2 * w + 2)
                    dve.tensor_tensor(sq_real[:, w], sq_real[:, w], sq_imag[:], ALU.add).then_inc(sum_ready, 1)

                def transposed_lo(tile, xt, hi_done, ready):
                    for k in range(2):
                        wait(dve, hi_done, tile, 2, k + 1)
                        dve.tensor_tensor(xt[:, 1, 2 * k:2 * k + 2].rearrange("p f t -> p (f t)"), gen[:, k, :],
                                          xt[:, 0, 2 * k:2 * k + 2].rearrange("p f t -> p (f t)").bitcast(F32),
                                          ALU.subtract).then_inc(ready, 1)

                if ffn.exists:
                    add_squares(0)
                if t1.exists:
                    transposed_lo(t1, xt1, xt1_hi, xt1_ready)
                if ffn.exists:
                    add_squares(1)
                if s.exists:
                    transposed_lo(s, xt2, xt2_hi, xt2_ready)

            steps(dve, step)

        @block.tensor
        def _(pe):
            def product3(out_, left, right, k_tiles):
                for f in range(k_tiles):
                    for n, (a, b) in enumerate(((0, 0), (0, 1), (1, 0))):
                        last = pe.matmul(out_, left(a, f), right(b, f), start=(f == 0 and n == 0),
                                         stop=(f == k_tiles - 1 and n == 2))
                return last

            pe.wait_ge(consts_made, CONSTS)
            pe.wait_ge(ctx_loaded, 16)
            for c in range(CT):
                for b in range(NB):
                    last = pe.transpose(gen[:, c, LK * b:LK * (b + 1)], ctx_in[:, b, P * c:P * (c + 1)], ident[:])
                last.then_inc(ctxt_mm, 1)
            pe.wait_ge(ctxt_ready, CT)
            pe.wait_ge(wk_loaded, 16)
            for g in range(NG):
                for c in range(CT):
                    last = pe.matmul(gen[:, g, :], raw[0][:, c, P * g:P * (g + 1)], ctx_t[:, c, :],
                                     start=(c == 0), stop=(c == CT - 1))
                last.then_inc(kt_mm, 1)
            pe.wait_ge(wv_loaded, 16)
            for b in range(NB):
                pe.wait_ge(ktlo_ready, b + 1)
                for c in range(CT):
                    last = pe.matmul(gen[:, b, :], ctx_t[:, c, LK * b:LK * (b + 1)], raw[1][:, c, :],
                                     start=(c == 0), stop=(c == CT - 1))
                last.then_inc(v_mm, 1)
            pe.wait_ge(v_ready, NB)
            pe.wait_ge(wlo_ready, 4)

            def step(s):
                q_tile, t1, ffn = s + 1, s + 2, s + -1

                def pair_scores(k):
                    g, j0 = k // 2, 2 * (k % 2)
                    wait(pe, exp_done, s, PAIRS, k - 1)
                    for i in range(2):
                        last = pe.matmul(scores[:, k % 2, i], kstack[0:KROWS, j0 + i, g, s.batch],
                                         qstack[0:KROWS, j0 + i, g], start=True, stop=True)
                    last.then_inc(st_mm, 1)

                def values(g):
                    wait(pe, exp_done, s, PAIRS, 2 * g + 2)
                    wait(pe, att_done, s, NG, g - 1)
                    for part in range(2):
                        for j in range(HG):
                            h = HG * g + j
                            last = pe.matmul(values_sums[HD * j:HD * (j + 1), g % 2, part],
                                             ones[:] if part else v_sb[:, s.batch, HD * h:HD * (h + 1)],
                                             probs[:, (2 * g + j // 2) % 4, j % 2], start=True, stop=True,
                                             tile_position=(0, HD * j))
                    last.then_inc(pv_mm, 1)

                if s.exists:
                    wait(pe, qstack_loaded, s, 16 * 3 * HG, 16 * 3 * HG)
                    wait(pe, negmax_loaded, s, 16, 16)
                    pair_scores(0)
                    pair_scores(1)
                    for g in range(NG):
                        if g + 1 < NG:
                            pair_scores(2 * g + 2)
                            pair_scores(2 * g + 3)
                        values(g)
                if q_tile.exists:
                    wait(pe, xt1_ready, q_tile, 2, 2)
                    for k in range(2):
                        if k == 0:
                            wait(pe, xt2_ready, ffn, 2, 2)
                        else:
                            wait(pe, negmax_ready, s, 1, 1)
                        for i in range(2):
                            g = 2 * k + i
                            last = product3(gen[:, 1 + k, T * i:T * (i + 1)],
                                            lambda a, f: wq[:, a, f, P * g:P * (g + 1)],
                                            lambda b, f: xt1[:, b, f], FT)
                        last.then_inc(q_mm, 1)
                if s.exists:
                    wait(pe, att_ready, s, NG, NG)
                    for w in range(SUB):
                        if w == 0:
                            wait(pe, sq_done, s + -2, 2 * SUB, 2 * SUB)
                        else:
                            wait(pe, xt2_ready, ffn, 2, 1)
                        product3(gen[:, (3, 0)[w], :], lambda a, f: att_t[:, a, f, P * w:P * (w + 1)],
                                 lambda b, f: wo[:, b, f], FT).then_inc(wo_mm, 1)
                if q_tile.exists:
                    wait(pe, kmask_ready, q_tile, 1, 1)
                    wait(pe, q_ready, q_tile, 2, 2)
                    for i in range(SUB * NG):
                        w, g = i // NG, i % NG
                        if i in (2, 3):
                            wait(pe, x2_ready, s, SUB, i - 1)
                        if i >= 4:
                            wait(pe, max_ready, q_tile, SUB * NG, i - 3)
                        pe.matmul(gen[:, (1, 2, 3, 0)[i % 4], :], qt[:, 0, g, P * w:P * (w + 1)],
                                  kmask[:, g].rearrange("p j k -> p (j k)"), start=True, stop=True).then_inc(smax_mm, 1)

                def feed_forward(u):
                    w, weights = u // 2, wsin if u % 2 else wcos
                    if q_tile.exists and u < 3:
                        wait(pe, max_ready, q_tile, SUB * NG, 5 + u)
                    if u == 2:
                        wait(pe, x2_ready, s, SUB, 1) if s.exists else None
                        wait(pe, sq_done, s + -2, 2 * SUB, 2 * SUB)
                    if u == 3:
                        wait(pe, sq_done, ffn, 2 * SUB, 3)
                    product3(gen[:, (1, 2, 3, 3)[u], :], lambda a, f: xt2[:, a, f, P * w:P * (w + 1)],
                             lambda b, f: weights[:, b, f], FT).then_inc(ffn_mm, 1)

                def transposes(part, done):
                    for k in range(2):
                        for f in (2 * k, 2 * k + 1):
                            for w in range(SUB):
                                at = T * (f % 2) + P * w
                                last = pe.transpose(gen[:, k, at:at + P], xn[:, part, w, P * f:P * (f + 1)], ident[:])
                        last.then_inc(done, 1)

                if ffn.exists:
                    wait(pe, xt2_ready, ffn, 2, 2)
                    for u in range(3):
                        feed_forward(u)
                if t1.exists:
                    wait(pe, xn1_ready, t1, 1, 1)
                    if q_tile.exists:
                        wait(pe, max_ready, q_tile, SUB * NG, SUB * NG)
                    if ffn.exists:
                        wait(pe, sq_done, ffn, 2 * SUB, 1)
                    transposes(0, tr1_mm)
                if q_tile.exists:
                    wait(pe, max_ready, q_tile, SUB * NG, SUB * NG)
                    if ffn.exists:
                        wait(pe, sq_done, ffn, 2 * SUB, 2)
                    for w in range(SUB):
                        last = pe.transpose(gen[0:NH, 2, P * w:P * (w + 1)], rowmax[:, w], ident[:])
                    last.then_inc(maxt_mm, 1)
                if ffn.exists:
                    feed_forward(3)
                if s.exists:
                    wait(pe, xn2_ready, s, 1, 1)
                    if t1.exists:
                        wait(pe, xt1_ready, t1, 2, 2)
                    transposes(1, tr2_mm)

            steps(pe, step)


_INS = ["x", "ctx_768", "L0_xattn_w_q", "L0_xattn_b_q", "L0_xattn_w_k", "L0_xattn_b_k", "L0_xattn_w_v",
        "L0_xattn_b_v", "L0_xattn_w_o", "L0_xattn_b_o", "L0_ffn_theta", "L0_ffn_phi",
        "L0_ffn_theta_noise", "L0_ffn_phi_noise"]


def kernel(**inputs):
    import numpy as _np
    import concourse.bacc as _bacc
    from concourse import mybir as _mybir
    from concourse.bass_utils import run_bass_kernel_spmd as _run

    nc = _bacc.Bacc("TRN2", target_bir_lowering=False, num_devices=1)
    arrays, args = {}, []
    for name in _INS:
        a = _np.ascontiguousarray(inputs[name])
        arrays[f"in_{name}_dram"] = a
        args.append(nc.dram_tensor(f"in_{name}_dram", a.shape, _mybir.dt.from_np(a.dtype), kind="ExternalInput").ap())
    shape = _np.shape(inputs["x"])
    args.append(nc.dram_tensor("out_0_dram", shape, _mybir.dt.float32, kind="ExternalOutput").ap())
    xattn_ffn(nc, *args)
    r = _run(nc, [arrays], core_ids=[0])
    return r.results[0]["out_0_dram"]
```

```python
from contextlib import ExitStack

import concourse.bass as bass
from concourse import mybir

ALU = mybir.AluOpType
ACT = mybir.ActivationFunctionType
AX = mybir.AxisListType
F32 = mybir.dt.float32
F32R = mybir.dt.float32r

P = 128
NB = 4
LQ = 2048
LK = 128
D = 512
DC = 384
NH = 16
HD = D // NH
T = 256
SUB = T // P
NT = NB * LQ // T
FT = D // P
CT = DC // P
HG = P // HD
NG = NH // HG
PAIRS = NH // 2
SCALE = float(HD) ** -0.5
LN_EPS = 1e-5
KROWS = 3 * HD + 1
MAXROW = 3 * HD

PI = 3.14159265358979
TWO_PI_HI = 6.28125
TWO_PI_MID = 0.0019350051879882812
TWO_PI_LO = 2 * PI - TWO_PI_HI - TWO_PI_MID
ROUND = 1.5 * 2.0 ** 23
SIN_MAX = 3.1415925

CONSTS = 6
Q_BANK, WO_BANK, FFN_BANK, MAXT_BANK, TR1_BANK, TR2_BANK = (0, 1), (2, 3), (0, 1, 3, 2), 2, (0, 1), (3, 0)
EXP_LN_SET = "natural_log_exp_and_others"
ANGLE_STEPS = 8

FIRST = -2
LOOP_FIRST = 2
LOOP_TURNS = 7
LAST = NT + 1


class Tile:

    def __init__(self, turn, c):
        self.turn, self.c = turn, c
        self.static = isinstance(turn, int)

    def __add__(self, n):
        return Tile(self.turn, self.c + n)

    @property
    def exists(self):
        return not self.static or 0 <= self.c < NT

    @property
    def batch(self):
        return self.c % NB

    @property
    def chunk(self):
        return self.turn + self.c // NB

    def count(self, per, n):
        return self.turn * (NB * per) + (self.c * per + n)


def wait(eng, sem, tile, per, n):
    if not tile.static:
        eng.wait_ge(sem, tile.count(per, n))
    elif tile.c * per + n > 0:
        eng.wait_ge(sem, min(tile.c * per + n, NT * per))


def steps(eng, step):
    for c in range(FIRST, LOOP_FIRST):
        step(Tile(0, c))
    with eng.Fori(0, LOOP_TURNS) as turn:
        for c in range(LOOP_FIRST, LOOP_FIRST + NB):
            step(Tile(turn, c))
    for c in range(LOOP_FIRST + NB * LOOP_TURNS, LAST + 1):
        step(Tile(0, c))



def xattn_ffn(nc, x, ctx_768, w_q, b_q, w_k, b_k, w_v, b_v, w_o, b_o, theta, phi, theta_noise, phi_noise, out):
    with ExitStack() as stack:
        def sb(name, shape, dt=F32):
            return stack.enter_context(nc.sbuf_tensor(name, shape, dt))

        def ps(name, shape):
            return stack.enter_context(nc.psum_tensor(name, shape, F32))

        def sem(name):
            return stack.enter_context(nc.semaphore(name))

        ident = sb("ident", [P, P])
        ones = sb("ones", [P, HD])
        wq = sb("wq", [P, 2, FT, D], F32R)
        wo = sb("wo", [P, 2, FT, D], F32R)
        wcos = sb("wcos", [P, 2, FT, D], F32R)
        wsin = sb("wsin", [P, 2, FT, D], F32R)
        kstack = sb("kstack", [P, HG, NG, NB, LK], F32R)
        v_sb = sb("v_sb", [P, NB, D])
        bq_col = sb("bq_col", [P, FT])
        bk_col = sb("bk_col", [P, FT])
        bo_row = sb("bo_row", [P, D])
        spare = sb("spare", [P, 1])
        minus_half = sb("minus_half", [P, 2 * SUB])

        eps = sb("eps", [P, 2 * SUB])

        kmask = sb("kmask", [P, NG, HG, LK], F32R)
        xres = sb("xres", [P, NB, SUB, D])
        xn = sb("xn", [P, 2, SUB, D])
        xt1 = sb("xt1", [P, 2, FT, T], F32R)
        xt2 = sb("xt2", [P, 2, FT, T], F32R)
        qt = sb("qt", [P, 2, NG, T], F32R)
        qstack = sb("qstack", [P, HG, NG, T], F32R)
        probs = sb("probs", [P, 4, 2, T])
        rden = sb("rden", [P, 2, T])
        att = sb("att", [P, T])
        att_t = sb("att_t", [P, 2, FT, T], F32R)
        sq_real = sb("sq_real", [P, SUB, D])
        sq_imag = sb("sq_imag", [P, D])
        stats = sb("stats", [P, 2 * SUB, 6])
        meanvar = sb("meanvar", [P, 2 * SUB, 2])
        vareps = sb("vareps", [P, 2 * SUB])
        rstd = sb("rstd", [P, 2 * SUB])
        rowmax = sb("rowmax", [P, SUB, NH])
        negmax = sb("negmax", [NH, T], F32R)

        ctx_in = probs[:].rearrange("p a b n -> p (a b n)")[:, 0:NB * DC].rearrange("p (b c) -> p b c", b=NB)
        ctx_t = xn[:].rearrange("p a s d -> p (a s) d")[:, 0:CT, :]
        bv_row = sq_imag
        raw = [xres[:, 2 * i:2 * i + 2].rearrange("p b s d -> p (b s) d") for i in range(2)]
        raw += [probs[:].rearrange("p a b n -> p (a b n)").rearrange("p (f d) -> p f d", f=FT),
                xn[:].rearrange("p a s d -> p (a s) d")]
        kt_hi = xt1[:].rearrange("p a f t -> p (a f t)").rearrange("p (g b k) -> p g b k", g=NG, b=NB)
        kt_lo = xt2[:].rearrange("p a f t -> p (a f t)").rearrange("p (g b k) -> p g b k", g=NG, b=NB)

        gen = ps("gen", [P, 4, 512])
        scores = ps("scores", [P, 2, 2, T])
        values_sums = ps("values_sums", [P, 2, 2, T])

        consts_made = sem("consts_made")
        passed = sem("passed")
        ident_zero = sem("ident_zero")
        ctx_loaded = sem("ctx_loaded")
        wk_loaded = sem("wk_loaded")
        wv_loaded = sem("wv_loaded")
        bias_loaded = sem("bias_loaded")
        raw_loaded = [sem(f"raw{i}_loaded") for i in range(4)]
        ctxt_mm = sem("ctxt_mm")
        ctxt_ready = sem("ctxt_ready")
        kt_mm = sem("kt_mm")
        kthi_ready = sem("kthi_ready")
        ktlo_ready = sem("ktlo_ready")
        v_mm = sem("v_mm")
        v_ready = sem("v_ready")
        kstack_loaded = sem("kstack_loaded")
        whi_ready = sem("whi_ready")
        wlo_ready = sem("wlo_ready")
        angle_step = sem("angle_step")
        trig_ready = sem("trig_ready")
        x_loaded = [sem(f"x_loaded{b}") for b in range(NB)]
        out_stored = [sem(f"out_stored{b}") for b in range(NB)]
        bn_done = sem("bn_done")
        bn2_done = sem("bn2_done")
        stats1_ready = sem("stats1_ready")
        stats2_ready = sem("stats2_ready")
        vareps1_ready = sem("vareps1_ready")
        vareps2_ready = sem("vareps2_ready")
        rstd1_ready = sem("rstd1_ready")
        rstd2_ready = sem("rstd2_ready")
        xn1_ready = sem("xn1_ready")
        xn2_ready = sem("xn2_ready")
        xb_ready = sem("xb_ready")
        tr1_mm = sem("tr1_mm")
        xt1_hi = sem("xt1_hi")
        xt1_ready = sem("xt1_ready")
        q_mm = sem("q_mm")
        q_hi = sem("q_hi")
        q_ready = sem("q_ready")
        qstack_loaded = sem("qstack_loaded")
        kmask_ready = sem("kmask_ready")
        smax_mm = sem("smax_mm")
        max_ready = sem("max_ready")
        maxt_mm = sem("maxt_mm")
        negmax_ready = sem("negmax_ready")
        negmax_loaded = sem("negmax_loaded")
        st_mm = sem("st_mm")
        exp_done = sem("exp_done")
        pv_mm = sem("pv_mm")
        logden_done = sem("logden_done")
        rden_ready = sem("rden_ready")
        att_done = sem("att_done")
        att_hi = sem("att_hi")
        att_ready = sem("att_ready")
        wo_mm = sem("wo_mm")
        x2_ready = sem("x2_ready")
        tr2_mm = sem("tr2_mm")
        xt2_hi = sem("xt2_hi")
        xt2_ready = sem("xt2_ready")
        ffn_mm = sem("ffn_mm")
        sq_done = sem("sq_done")
        sum_ready = sem("sum_ready")
        root_ready = sem("root_ready")
        exp_table = sem("exp_table")
        result_ready = sem("result_ready")

        x_tiles = x.rearrange("b (i p s) f -> b i p s f", p=P, s=SUB)
        out_tiles = out.rearrange("b (i p s) f -> b i p s f", p=P, s=SUB)

        def rows(w):
            return w.rearrange("(f p) n -> p f n", p=P)

        def smax_bank(i):
            bank = (scores, values_sums)[i % 4 // 2][:, i % 2]
            return bank.rearrange("p a t -> p (a t)")

        block = stack.enter_context(nc.Block())

        @block.sync
        def _(sp):
            sp.dma_start(ctx_in, ctx_768.rearrange("b p c -> p b c")).then_inc(ctx_loaded, 16)
            sp.dma_start(raw[0][:, 0:CT, :], rows(w_k)).then_inc(wk_loaded, 16)
            sp.dma_start(raw[1][:, 0:CT, :], rows(w_v)).then_inc(wv_loaded, 16)
            sp.dma_start(bq_col[:], b_q.rearrange("(f p) -> p f", p=P), allow_slow_non_contiguous=True).then_inc(bias_loaded, 16)
            sp.dma_start(bk_col[:], b_k.rearrange("(f p) -> p f", p=P), allow_slow_non_contiguous=True).then_inc(bias_loaded, 16)
            sp.dma_start(bv_row[:], b_v.partition_broadcast(P)).then_inc(bias_loaded, 16)
            sp.dma_start(bo_row[:], b_o.partition_broadcast(P)).then_inc(bias_loaded, 16)
            sp.wait_ge(ctxt_mm, CT)
            sp.dma_start(raw[2], rows(w_q)).then_inc(raw_loaded[2], 16)
            sp.wait_ge(kt_mm, NG)
            sp.dma_start(raw[0], rows(theta)).then_inc(raw_loaded[0], 16)
            sp.wait_ge(v_mm, NB)
            sp.dma_start(raw[1], rows(theta_noise)).then_inc(raw_loaded[1], 16)
            sp.dma_start(raw[3], rows(w_o)).then_inc(raw_loaded[3], 16)
            sp.wait_ge(kthi_ready, NG)
            sp.wait_ge(ktlo_ready, NG)
            for j in range(HG):
                for i, part in enumerate((kt_hi, kt_hi, kt_lo)):
                    sp.dma_start(kstack[HD * i:HD * (i + 1), j].bitcast(F32),
                                 part[HD * j:HD * (j + 1)].bitcast(F32)).then_inc(kstack_loaded, 16)
            sp.wait_ge(wlo_ready, 2)
            sp.dma_start(raw[2], rows(phi)).then_inc(raw_loaded[2], 16)
            sp.dma_start(raw[3], rows(phi_noise)).then_inc(raw_loaded[3], 16)
            sp.wait_ge(wlo_ready, 3)

            def step(s):
                new, done, load = s + 1, s + -2, s + 2
                if done.exists:
                    wait(sp, result_ready, done, SUB, SUB)
                    sp.sem_inc(passed, 1)
                    sp.dma_start(out_tiles[done.batch, done.chunk], xres[:, done.batch]).then_inc(out_stored[done.batch], 16)
                if load.exists:
                    if done.exists:
                        sp.wait_ge(out_stored[done.batch], 16 * (done.chunk + 1))
                        sp.sem_inc(passed, 1)
                    sp.dma_start(xres[:, load.batch], x_tiles[load.batch, load.chunk]).then_inc(x_loaded[load.batch], 16)
                if new.exists:
                    wait(sp, q_ready, new, 2, 2)
                    sp.sem_inc(passed, 1)
                    wait(sp, st_mm, s, PAIRS, PAIRS)
                    for j in range(HG):
                        for i, part in enumerate((0, 1, 0)):
                            sp.dma_start(qstack[HD * i:HD * (i + 1), j].bitcast(F32),
                                         qt[HD * j:HD * (j + 1), part].bitcast(F32)).then_inc(qstack_loaded, 16)
                    wait(sp, negmax_ready, new, 1, 1)
                    sp.dma_start(qstack[MAXROW:MAXROW + 1].rearrange("p j g t -> p (j g) t").bitcast(F32),
                                 negmax[:].bitcast(F32)).then_inc(negmax_loaded, 16)

            steps(sp, step)
            for b in range(NB):
                sp.wait_ge(out_stored[b], 16 * NT // NB)

        @block.gpsimd
        def _(pool):
            pool.memset(ident[:], 0.0).then_inc(ident_zero, 1)
            pool.wait_ge(ident_zero, 1)
            pool.affine_select(out=ident[:], in_=ident[:], compare_op=ALU.not_equal, fill=1.0, base=0,
                               pattern=[[-1, P]], channel_multiplier=1).then_inc(consts_made, 1)
            pool.memset(ones[:], 1.0).then_inc(consts_made, 1)
            pool.memset(minus_half[:], -0.5).then_inc(consts_made, 1)
            pool.memset(eps[:], LN_EPS).then_inc(consts_made, 1)
            pool.wait_ge(consts_made, 4)
            pool.memset(kstack[MAXROW:MAXROW + 1].bitcast(F32), 1.0).then_inc(consts_made, 1)
            pool.wait_ge(consts_made, 5)
            pool.memset(kmask[:].bitcast(F32), 0.0).then_inc(consts_made, 1)
            pool.wait_ge(consts_made, CONSTS)
            pool.wait_ge(bias_loaded, 64)

            def step(s):
                new, done = s + 2, s + -2

                def inverse_deviation(tile, part, stats_ready, vareps_ready, rstd_ready, xn_ready):
                    r = slice(SUB * part, SUB * (part + 1))
                    wait(pool, xn_ready, tile, 1, 0)
                    wait(pool, stats_ready, tile, 1, 1)
                    pool.tensor_tensor(vareps[:, r], meanvar[:, r, 1], eps[:, r], ALU.add).then_inc(vareps_ready, 1)
                    wait(pool, vareps_ready, tile, 1, 1)
                    pool.tensor_tensor(rstd[:, r], vareps[:, r], minus_half[:, r], ALU.pow).then_inc(rstd_ready, 1)

                if done.exists:
                    wait(pool, root_ready, done, 1, 1)
                    for w in range(SUB):
                        pool.tensor_tensor(xres[:, done.batch, w], xres[:, done.batch, w], sq_real[:, w],
                                           ALU.add).then_inc(result_ready, 1)
                if s.exists:
                    inverse_deviation(s, 1, stats2_ready, vareps2_ready, rstd2_ready, xn2_ready)
                if new.exists:
                    inverse_deviation(new, 0, stats1_ready, vareps1_ready, rstd1_ready, xn1_ready)
                    wait(pool, xn1_ready, new, 1, 1)
                    for w in range(SUB):
                        last = pool.tensor_tensor(xres[:, new.batch, w], xres[:, new.batch, w], bo_row[:], ALU.add)
                    last.then_inc(xb_ready, 1)

            steps(pool, step)

        @block.scalar
        def _(act):
            for c in range(CT):
                act.wait_ge(ctxt_mm, c + 1)
                act.activation(ctx_t[:, c, :], gen[:, c, :], ACT.Copy).then_inc(ctxt_ready, 1)
            act.wait_ge(bias_loaded, 64)
            for g in range(NG):
                act.wait_ge(kt_mm, g + 1)
                act.activation(kt_hi[:, g].rearrange("p b k -> p (b k)"), gen[:, g, :], ACT.Identity,
                               bias=bk_col[:, g:g + 1]).then_inc(kthi_ready, 1)
            for i, (src, w) in enumerate(((2, wq), (3, wo))):
                act.wait_ge(raw_loaded[src], 16)
                act.activation(w[:, 0], raw[src], ACT.Copy).then_inc(whi_ready, 1)
            for i, (src, w) in enumerate(((0, wcos), (2, wsin))):
                act.wait_ge(angle_step, ANGLE_STEPS * (i + 1))
                act.activation(raw[src], raw[src], ACT.Sin).then_inc(trig_ready, 1)
                act.wait_ge(trig_ready, i + 1)
                act.activation(w[:, 0], raw[src], ACT.Copy).then_inc(whi_ready, 1)
            act.wait_ge(kstack_loaded, 16 * 3 * HG)
            act.wait_ge(consts_made, CONSTS)
            act.preload_act_table_set(EXP_LN_SET)

            def step(s):
                q_tile, t1, ffn, done = s + 1, s + 2, s + -1, s + -2

                def exps(k):
                    wait(act, st_mm, s, PAIRS, k + 1)
                    wait(act, pv_mm, s, NG, k // 2 - 1)
                    act.activation(probs[:, k % 4], scores[:, k % 2], ACT.Exp, scale=SCALE).then_inc(exp_done, 1)

                def inverse_sums(g):
                    wait(act, pv_mm, s, NG, g + 1)
                    wait(act, att_done, s, NG, g - 1)
                    act.activation(rden[:, g % 2], values_sums[:, g % 2, 1], ACT.Ln).then_inc(logden_done, 1)
                    wait(act, logden_done, s, NG, g + 1)
                    act.activation(rden[:, g % 2], rden[:, g % 2], ACT.Exp, scale=-1.0).then_inc(rden_ready, 1)

                def square(u):
                    wait(act, ffn_mm, ffn, 2 * SUB, u + 1)
                    if u == 0:
                        wait(act, result_ready, ffn, SUB, 0)
                    if u % 2:
                        wait(act, sum_ready, ffn, SUB, u // 2)
                    act.activation(sq_imag[:] if u % 2 else sq_real[:, u // 2], gen[:, FFN_BANK[u], :],
                                   ACT.Square).then_inc(sq_done, 1)

                if s.exists:
                    for k in range(4):
                        exps(k)
                    for g in range(NG):
                        inverse_sums(g)
                        if g + 2 < NG:
                            exps(2 * g + 4)
                            exps(2 * g + 5)
                if done.exists:
                    wait(act, sum_ready, done, SUB, SUB)
                    act.activation(sq_real[:], sq_real[:], ACT.Sqrt).then_inc(root_ready, 1)
                    act.preload_act_table_set(EXP_LN_SET)
                if q_tile.exists:
                    wait(act, qstack_loaded, s, 16 * 3 * HG, 16 * 3 * HG)
                    wait(act, smax_mm, s, SUB * NG, SUB * NG)
                    for k in range(2):
                        wait(act, q_mm, q_tile, 2, k + 1)
                        for i in range(2):
                            g = 2 * k + i
                            last = act.activation(qt[:, 0, g], gen[:, Q_BANK[k], T * i:T * (i + 1)], ACT.Identity,
                                                  bias=bq_col[:, g:g + 1])
                        last.then_inc(q_hi, 1)
                if ffn.exists:
                    square(0)
                    square(1)
                if q_tile.exists:
                    wait(act, maxt_mm, q_tile, 1, 1)
                    wait(act, negmax_loaded, s, 16, 16)
                    act.activation(negmax[:], gen[0:NH, MAXT_BANK, 0:T], ACT.Copy, scale=-1.0).then_inc(negmax_ready, 1)
                if t1.exists:
                    wait(act, smax_mm, q_tile, SUB * NG, SUB * NG)
                    for j in range(HG):
                        last = act.activation(kmask[HD * j:HD * (j + 1), :, j, :],
                                              kstack[0:HD, j, :, t1.batch, :].bitcast(F32), ACT.Copy)
                    last.then_inc(kmask_ready, 1)
                if ffn.exists:
                    square(2)

                def transposed_hi(tile, xt, banks, done, ready):
                    for k in range(2):
                        wait(act, done, tile, 2, k + 1)
                        act.activation(xt[:, 0, 2 * k:2 * k + 2].rearrange("p f t -> p (f t)"), gen[:, banks[k], :],
                                       ACT.Copy).then_inc(ready, 1)

                if t1.exists:
                    wait(act, q_mm, q_tile, 2, 2)
                    transposed_hi(t1, xt1, TR1_BANK, tr1_mm, xt1_hi)
                if ffn.exists:
                    square(3)
                if s.exists:
                    wait(act, ffn_mm, ffn, 2 * SUB, 2 * SUB)
                    transposed_hi(s, xt2, TR2_BANK, tr2_mm, xt2_hi)

            steps(act, step)

        @block.vector
        def _(dve):
            dve.wait_ge(bias_loaded, 64)
            for g in range(NG):
                dve.wait_ge(kthi_ready, g + 1)
                dve.scalar_tensor_tensor(kt_lo[:, g].rearrange("p b k -> p (b k)"), gen[:, g, :], bk_col[:, g:g + 1],
                                         kt_hi[:, g].rearrange("p b k -> p (b k)").bitcast(F32),
                                         ALU.add, ALU.subtract).then_inc(ktlo_ready, 1)
            for b in range(NB):
                dve.wait_ge(v_mm, b + 1)
                dve.tensor_tensor(v_sb[:, b], gen[:, b, :], bv_row[:], ALU.add).then_inc(v_ready, 1)
            for i, (src, w) in enumerate(((2, wq), (3, wo))):
                dve.wait_ge(whi_ready, i + 1)
                dve.tensor_tensor(w[:, 1], raw[src], w[:, 0].bitcast(F32), ALU.subtract).then_inc(wlo_ready, 1)
            for i, (a, b, offset, w) in enumerate(((0, 1, PI / 2, wcos), (2, 3, 0.0, wsin))):
                y, k = raw[a], raw[b]
                n = ANGLE_STEPS * i
                dve.wait_ge(raw_loaded[a], 16 if a < 2 else 32)
                dve.wait_ge(raw_loaded[b], 16 if b < 2 else 32)
                dve.tensor_tensor(y, y, k, ALU.add).then_inc(angle_step, 1)
                dve.wait_ge(angle_step, n + 1)
                dve.tensor_scalar(k, y, 1.0 / (2 * PI), offset / (2 * PI), ALU.mult, ALU.add).then_inc(angle_step, 1)
                dve.wait_ge(angle_step, n + 2)
                dve.tensor_scalar(k, k, ROUND, ROUND, ALU.add, ALU.subtract).then_inc(angle_step, 1)
                for m, part in enumerate((TWO_PI_HI, TWO_PI_MID, TWO_PI_LO)):
                    dve.wait_ge(angle_step, n + 3 + m)
                    dve.scalar_tensor_tensor(y, k, -part, y, ALU.mult, ALU.add).then_inc(angle_step, 1)
                dve.wait_ge(angle_step, n + 6)
                dve.tensor_scalar(y, y, offset, SIN_MAX, ALU.add, ALU.min).then_inc(angle_step, 1)
                dve.wait_ge(angle_step, n + 7)
                dve.tensor_scalar(y, y, -SIN_MAX, None, ALU.max).then_inc(angle_step, 1)
                dve.wait_ge(whi_ready, 3 + i)
                dve.tensor_tensor(w[:, 1], raw[a], w[:, 0].bitcast(F32), ALU.subtract).then_inc(wlo_ready, 1)

            def step(s):
                q_tile, t1, ffn = s + 1, s + 2, s + -1

                def normalise(tile, part, transposed, rstd_ready, ready):
                    wait(dve, rstd_ready, tile, 1, 1)
                    wait(dve, transposed, tile, 2, 0)
                    for w in range(SUB):
                        r = SUB * part + w
                        last = dve.tensor_scalar(xn[:, part, w], xres[:, tile.batch, w], meanvar[:, r, 0:1],
                                                 rstd[:, r:r + 1], ALU.subtract, ALU.mult)
                    last.then_inc(ready, 1)

                def aggregate(tile, part, done, ready):
                    wait(dve, done, tile, SUB, SUB)
                    dve.sem_inc(passed, 1)
                    for w in range(SUB):
                        last = dve.bn_aggr(meanvar[:, SUB * part + w], stats[:, SUB * part + w])
                    last.then_inc(ready, 1)

                def maxima(some):
                    for i in some:
                        w, g = i // NG, i % NG
                        wait(dve, smax_mm, q_tile, SUB * NG, i + 1)
                        dve.tensor_reduce(rowmax[:, w].rearrange("p (j g) -> p g j", g=NG)[:, g],
                                          smax_bank(i).rearrange("p (j k) -> p j k", j=HG),
                                          AX.X, ALU.max).then_inc(max_ready, 1)

                def add_squares(w):
                    wait(dve, sq_done, ffn, 2 * SUB, 2 * w + 2)
                    dve.tensor_tensor(sq_real[:, w], sq_real[:, w], sq_imag[:], ALU.add).then_inc(sum_ready, 1)

                def transposed_lo(tile, xt, banks, hi_done, ready):
                    for k in range(2):
                        wait(dve, hi_done, tile, 2, k + 1)
                        dve.tensor_tensor(xt[:, 1, 2 * k:2 * k + 2].rearrange("p f t -> p (f t)"), gen[:, banks[k], :],
                                          xt[:, 0, 2 * k:2 * k + 2].rearrange("p f t -> p (f t)").bitcast(F32),
                                          ALU.subtract).then_inc(ready, 1)

                if s.exists:
                    wait(dve, wo_mm, s, SUB, 0)
                    for g in range(NG):
                        wait(dve, rden_ready, s, NG, g + 1)
                        wait(dve, att_ready, s, NG, g)
                        dve.tensor_tensor(att[:], values_sums[:, g % 2, 0], rden[:, g % 2], ALU.mult).then_inc(att_done, 1)
                        wait(dve, att_done, s, NG, g + 1)
                        dve.tensor_copy(att_t[:, 0, g], att[:]).then_inc(att_hi, 1)
                        wait(dve, att_hi, s, NG, g + 1)
                        dve.tensor_tensor(att_t[:, 1, g], att[:], att_t[:, 0, g].bitcast(F32),
                                          ALU.subtract).then_inc(att_ready, 1)
                if q_tile.exists:
                    for k in range(2):
                        wait(dve, q_hi, q_tile, 2, k + 1)
                        for i in range(2):
                            g = 2 * k + i
                            last = dve.scalar_tensor_tensor(qt[:, 1, g], gen[:, Q_BANK[k], T * i:T * (i + 1)],
                                                            bq_col[:, g:g + 1], qt[:, 0, g].bitcast(F32),
                                                            ALU.add, ALU.subtract)
                        last.then_inc(q_ready, 1)
                if s.exists:
                    wait(dve, xb_ready, s, 1, 1)
                    for w in range(SUB):
                        wait(dve, wo_mm, s, SUB, w + 1)
                        dve.tensor_tensor(xres[:, s.batch, w], gen[:, WO_BANK[w], :], xres[:, s.batch, w],
                                          ALU.add).then_inc(x2_ready, 1)
                        wait(dve, x2_ready, s, SUB, w + 1)
                        dve.bn_stats(stats[:, SUB + w], xres[:, s.batch, w]).then_inc(bn2_done, 1)
                    aggregate(s, 1, bn2_done, stats2_ready)
                if q_tile.exists:
                    wait(dve, maxt_mm, s, 1, 1)
                    maxima(range(4))
                if t1.exists:
                    dve.wait_ge(x_loaded[t1.batch], 16 * (t1.chunk + 1))
                    for w in range(SUB):
                        dve.bn_stats(stats[:, w], xres[:, t1.batch, w]).then_inc(bn_done, 1)
                    aggregate(t1, 0, bn_done, stats1_ready)
                if q_tile.exists:
                    maxima(range(4, SUB * NG))
                if t1.exists:
                    normalise(t1, 0, tr1_mm, rstd1_ready, xn1_ready)
                if s.exists:
                    normalise(s, 1, tr2_mm, rstd2_ready, xn2_ready)
                if ffn.exists:
                    add_squares(0)
                if t1.exists:
                    transposed_lo(t1, xt1, TR1_BANK, xt1_hi, xt1_ready)
                if ffn.exists:
                    add_squares(1)
                if s.exists:
                    transposed_lo(s, xt2, TR2_BANK, xt2_hi, xt2_ready)

            steps(dve, step)

        @block.tensor
        def _(pe):
            def product3(out_, left, right, k_tiles):
                for f in range(k_tiles):
                    for n, (a, b) in enumerate(((0, 0), (0, 1), (1, 0))):
                        last = pe.matmul(out_, left(a, f), right(b, f), start=(f == 0 and n == 0),
                                         stop=(f == k_tiles - 1 and n == 2))
                return last

            pe.wait_ge(consts_made, CONSTS)
            pe.wait_ge(ctx_loaded, 16)
            for c in range(CT):
                for b in range(NB):
                    last = pe.transpose(gen[:, c, LK * b:LK * (b + 1)], ctx_in[:, b, P * c:P * (c + 1)], ident[:])
                last.then_inc(ctxt_mm, 1)
            pe.wait_ge(ctxt_ready, CT)
            pe.wait_ge(wk_loaded, 16)
            for g in range(NG):
                for c in range(CT):
                    last = pe.matmul(gen[:, g, :], raw[0][:, c, P * g:P * (g + 1)], ctx_t[:, c, :],
                                     start=(c == 0), stop=(c == CT - 1))
                last.then_inc(kt_mm, 1)
            pe.wait_ge(wv_loaded, 16)
            for b in range(NB):
                pe.wait_ge(ktlo_ready, b + 1)
                for c in range(CT):
                    last = pe.matmul(gen[:, b, :], ctx_t[:, c, LK * b:LK * (b + 1)], raw[1][:, c, :],
                                     start=(c == 0), stop=(c == CT - 1))
                last.then_inc(v_mm, 1)
            pe.wait_ge(v_ready, NB)
            pe.wait_ge(wlo_ready, 4)

            def step(s):
                q_tile, t1, ffn = s + 1, s + 2, s + -1

                def pair_scores(k):
                    g, j0 = k // 2, 2 * (k % 2)
                    wait(pe, exp_done, s, PAIRS, k - 1)
                    for i in range(2):
                        last = pe.matmul(scores[:, k % 2, i], kstack[0:KROWS, j0 + i, g, s.batch],
                                         qstack[0:KROWS, j0 + i, g], start=True, stop=True)
                    last.then_inc(st_mm, 1)

                def values(g):
                    wait(pe, exp_done, s, PAIRS, 2 * g + 2)
                    wait(pe, att_done, s, NG, g - 1)
                    for part in range(2):
                        for j in range(HG):
                            h = HG * g + j
                            last = pe.matmul(values_sums[HD * j:HD * (j + 1), g % 2, part],
                                             ones[:] if part else v_sb[:, s.batch, HD * h:HD * (h + 1)],
                                             probs[:, (2 * g + j // 2) % 4, j % 2], start=True, stop=True,
                                             tile_position=(0, HD * j))
                    last.then_inc(pv_mm, 1)

                if s.exists:
                    wait(pe, qstack_loaded, s, 16 * 3 * HG, 16 * 3 * HG)
                    wait(pe, negmax_loaded, s, 16, 16)
                    pair_scores(0)
                    pair_scores(1)
                    for g in range(NG):
                        if g + 1 < NG:
                            pair_scores(2 * g + 2)
                            pair_scores(2 * g + 3)
                        values(g)
                if q_tile.exists:
                    wait(pe, xt1_ready, q_tile, 2, 2)
                    wait(pe, xt2_ready, ffn, 2, 2)
                    for k in range(2):
                        for i in range(2):
                            g = 2 * k + i
                            last = product3(gen[:, Q_BANK[k], T * i:T * (i + 1)],
                                            lambda a, f: wq[:, a, f, P * g:P * (g + 1)],
                                            lambda b, f: xt1[:, b, f], FT)
                        last.then_inc(q_mm, 1)
                if s.exists:
                    wait(pe, att_ready, s, NG, NG)
                    wait(pe, sq_done, s + -2, 2 * SUB, 2 * SUB)
                    wait(pe, xt2_ready, ffn, 2, 1)
                    for w in range(SUB):
                        product3(gen[:, WO_BANK[w], :], lambda a, f: att_t[:, a, f, P * w:P * (w + 1)],
                                 lambda b, f: wo[:, b, f], FT).then_inc(wo_mm, 1)

                def scores_for_max(some):
                    for i in some:
                        w, g = i // NG, i % NG
                        if i >= 4:
                            wait(pe, max_ready, q_tile, SUB * NG, i - 3)
                        pe.matmul(smax_bank(i), qt[:, 0, g, P * w:P * (w + 1)],
                                  kmask[:, g].rearrange("p j k -> p (j k)"), start=True, stop=True).then_inc(smax_mm, 1)

                def feed_forward(u):
                    w, weights = u // 2, wsin if u % 2 else wcos
                    product3(gen[:, FFN_BANK[u], :], lambda a, f: xt2[:, a, f, P * w:P * (w + 1)],
                             lambda b, f: weights[:, b, f], FT).then_inc(ffn_mm, 1)

                def transposes(part, banks, done):
                    for k in range(2):
                        for f in (2 * k, 2 * k + 1):
                            for w in range(SUB):
                                at = T * (f % 2) + P * w
                                last = pe.transpose(gen[:, banks[k], at:at + P], xn[:, part, w, P * f:P * (f + 1)], ident[:])
                        last.then_inc(done, 1)

                if q_tile.exists:
                    wait(pe, kmask_ready, q_tile, 1, 1)
                    wait(pe, q_ready, q_tile, 2, 2)
                    wait(pe, att_done, s, NG, NG)
                    wait(pe, exp_done, s, PAIRS, PAIRS)
                    scores_for_max(range(4))
                if ffn.exists:
                    wait(pe, xt2_ready, ffn, 2, 2)
                    feed_forward(0)
                if q_tile.exists:
                    scores_for_max(range(4, SUB * NG))
                if ffn.exists:
                    feed_forward(1)
                if q_tile.exists:
                    wait(pe, max_ready, q_tile, SUB * NG, SUB * NG)
                    wait(pe, x2_ready, s, SUB, 1)
                    for w in range(SUB):
                        last = pe.transpose(gen[0:NH, MAXT_BANK, P * w:P * (w + 1)], rowmax[:, w], ident[:])
                    last.then_inc(maxt_mm, 1)
                if ffn.exists:
                    wait(pe, x2_ready, s, SUB, SUB)
                    feed_forward(2)
                if t1.exists:
                    wait(pe, xn1_ready, t1, 1, 1)
                    wait(pe, sq_done, ffn, 2 * SUB, 2)
                    transposes(0, TR1_BANK, tr1_mm)
                if ffn.exists:
                    wait(pe, negmax_ready, q_tile, 1, 1)
                    wait(pe, sq_done, s + -2, 2 * SUB, 2 * SUB)
                    feed_forward(3)
                if s.exists:
                    wait(pe, xn2_ready, s, 1, 1)
                    wait(pe, sq_done, ffn, 2 * SUB, 3)
                    if t1.exists:
                        wait(pe, xt1_ready, t1, 2, 1)
                    transposes(1, TR2_BANK, tr2_mm)

            steps(pe, step)


_INS = ["x", "ctx_768", "L0_xattn_w_q", "L0_xattn_b_q", "L0_xattn_w_k", "L0_xattn_b_k", "L0_xattn_w_v",
        "L0_xattn_b_v", "L0_xattn_w_o", "L0_xattn_b_o", "L0_ffn_theta", "L0_ffn_phi",
        "L0_ffn_theta_noise", "L0_ffn_phi_noise"]


def kernel(**inputs):
    import numpy as _np
    import concourse.bacc as _bacc
    from concourse import mybir as _mybir
    from concourse.bass_utils import run_bass_kernel_spmd as _run

    nc = _bacc.Bacc("TRN2", target_bir_lowering=False, num_devices=1)
    arrays, args = {}, []
    for name in _INS:
        a = _np.ascontiguousarray(inputs[name])
        arrays[f"in_{name}_dram"] = a
        args.append(nc.dram_tensor(f"in_{name}_dram", a.shape, _mybir.dt.from_np(a.dtype), kind="ExternalInput").ap())
    shape = _np.shape(inputs["x"])
    args.append(nc.dram_tensor("out_0_dram", shape, _mybir.dt.float32, kind="ExternalOutput").ap())
    xattn_ffn(nc, *args)
    r = _run(nc, [arrays], core_ids=[0])
    return r.results[0]["out_0_dram"]
```

```python
from contextlib import ExitStack

import concourse.bass as bass
from concourse import mybir

ALU = mybir.AluOpType
ACT = mybir.ActivationFunctionType
AX = mybir.AxisListType
F32 = mybir.dt.float32
F32R = mybir.dt.float32r

P = 128
NB = 4
LQ = 2048
LK = 128
D = 512
DC = 384
NH = 16
HD = D // NH
T = 256
SUB = T // P
NT = NB * LQ // T
FT = D // P
CT = DC // P
HG = P // HD
NG = NH // HG
PAIRS = NH // 2
SCALE = float(HD) ** -0.5
LN_EPS = 1e-5
KROWS = 3 * HD + 1
MAXROW = 3 * HD

PI = 3.14159265358979
TWO_PI_HI = 6.28125
TWO_PI_MID = 0.0019350051879882812
TWO_PI_LO = 2 * PI - TWO_PI_HI - TWO_PI_MID
TWO_PI_PARTS = (TWO_PI_HI, TWO_PI_MID, TWO_PI_LO)
ROUND = 1.5 * 2.0 ** 23
SIN_MAX = 3.1415925

CONSTS = 5
STACK_CONSTS = 2
Q_BANK, WO_BANK, FFN_BANK, MAXT_BANK, TR1_BANK, TR2_BANK = (0, 1), (2, 3), (0, 1, 3, 2), 2, (0, 1), (0, 3)
V_BANK = (2, 3, 2, 3)
EXP_LN_SET = "natural_log_exp_and_others"
ANGLE_TILES = 2 * FT
DVE_ANGLES, DVE_ANGLE_STEPS = (0, 1, 2, 3, 5), 6
POOL_ANGLES, POOL_ANGLE_STEPS = (4, 6, 7), 10
ANGLE_BUFFER = (0, 1, 2, 0, 1, 0, 1, 3)

FIRST = -2
LOOP_FIRST = 2
LOOP_TURNS = 7
LAST = NT + 1


class Tile:

    def __init__(self, turn, c):
        self.turn, self.c = turn, c
        self.static = isinstance(turn, int)

    def __add__(self, n):
        return Tile(self.turn, self.c + n)

    @property
    def exists(self):
        return not self.static or 0 <= self.c < NT

    @property
    def batch(self):
        return self.c % NB

    @property
    def chunk(self):
        return self.turn + self.c // NB

    def count(self, per, n):
        return self.turn * (NB * per) + (self.c * per + n)


def wait(eng, sem, tile, per, n):
    if not tile.static:
        eng.wait_ge(sem, tile.count(per, n))
    elif tile.c * per + n > 0:
        eng.wait_ge(sem, min(tile.c * per + n, NT * per))


def is_step(s, c):
    return s.static and s.c == c


def starts_early(tile):
    return not (tile.static and tile.c == 0)


def loaded_early(tile):
    return tile.static and 0 <= tile.c <= 2


def steps(eng, step):
    for c in range(FIRST, LOOP_FIRST):
        step(Tile(0, c))
    with eng.Fori(0, LOOP_TURNS) as turn:
        for c in range(LOOP_FIRST, LOOP_FIRST + NB):
            step(Tile(turn, c))
    for c in range(LOOP_FIRST + NB * LOOP_TURNS, LAST + 1):
        step(Tile(0, c))


def xattn_ffn(nc, x, ctx_768, w_q, b_q, w_k, b_k, w_v, b_v, w_o, b_o, theta, phi, theta_noise, phi_noise, out):
    with ExitStack() as stack:
        def sb(name, shape, dt=F32):
            return stack.enter_context(nc.sbuf_tensor(name, shape, dt))

        def ps(name, shape):
            return stack.enter_context(nc.psum_tensor(name, shape, F32))

        def sem(name):
            return stack.enter_context(nc.semaphore(name))

        ident = sb("ident", [P, P])
        ones = sb("ones", [P, HD])
        wq = sb("wq", [P, 2, FT, D], F32R)
        wo = sb("wo", [P, 2, FT, D], F32R)
        wcos = sb("wcos", [P, 2, FT, D], F32R)
        wsin = sb("wsin", [P, 2, FT, D], F32R)
        kstack = sb("kstack", [P, HG, NG, NB, LK], F32R)
        v_sb = sb("v_sb", [P, NB, D])
        bq_col = sb("bq_col", [P, FT])
        bk_col = sb("bk_col", [P, FT])
        bo_row = sb("bo_row", [P, D])
        half_pi = sb("half_pi", [P, 1])
        minus_half = sb("minus_half", [P, 2 * SUB])
        eps = sb("eps", [P, 2 * SUB])

        kmask = sb("kmask", [P, NG, HG, LK], F32R)
        xres = sb("xres", [P, NB, SUB, D])
        xn = sb("xn", [P, 2, SUB, D])
        xt1 = sb("xt1", [P, 2, FT, T], F32R)
        xt2 = sb("xt2", [P, 2, FT, T], F32R)
        qt = sb("qt", [P, 2, NG, T], F32R)
        qstack = sb("qstack", [P, HG, NG, T], F32R)
        probs = sb("probs", [P, 4, 2, T])
        rden = sb("rden", [P, 2, T])
        att = sb("att", [P, 2, T])
        att_t = sb("att_t", [P, 2, FT, T], F32R)
        squares = sb("squares", [P, SUB + 1, D])
        sq_real, sq_imag = squares[:, 0:SUB], squares[:, SUB]
        stats = sb("stats", [P, 2 * SUB, 6])
        meanvar = sb("meanvar", [P, 2 * SUB, 2])
        vareps = sb("vareps", [P, 2 * SUB])
        rstd = sb("rstd", [P, 2 * SUB])
        rowmax = sb("rowmax", [P, SUB, NH])
        negmax = sb("negmax", [NH, T], F32R)

        wk_in = v_sb[:].rearrange("p b d -> p (b d)")[:, 0:CT * D].rearrange("p (c d) -> p c d", c=CT)
        wv_in = (xres[:, 2, 0], xres[:, 2, 1], sq_imag)
        ctx_in = probs[:].rearrange("p a b n -> p (a b n)")[:, 0:NB * DC].rearrange("p (b c) -> p b c", b=NB)
        ctx_t = (xn[:, 1, 0], xn[:, 1, 1], rden[:].rearrange("p a t -> p (a t)"))
        bv_row = att[:].rearrange("p a t -> p (a t)")
        w_in = probs[:].rearrange("p a b n -> p (a b n)").rearrange("p (f d) -> p f d", f=FT)
        angle_in = [(squares[:, 0:2], xres[:, 3], xres[:, 1], xn[:, 1])[i] for i in ANGLE_BUFFER]
        kt_hi = att_t[:].rearrange("p a f t -> p (a f t)").rearrange("p (g b k) -> p g b k", g=NG, b=NB)
        kt_lo = xt2[:].rearrange("p a f t -> p (a f t)").rearrange("p (g b k) -> p g b k", g=NG, b=NB)

        gen = ps("gen", [P, 4, 512])
        scores = ps("scores", [P, 2, 2, T])
        values_sums = ps("values_sums", [P, 2, 2, T])

        consts_made = sem("consts_made")
        passed = sem("passed")
        ident_zero = sem("ident_zero")
        ctx_loaded = sem("ctx_loaded")
        wk_loaded = sem("wk_loaded")
        wv_loaded = sem("wv_loaded")
        bias_loaded = sem("bias_loaded")
        rows_loaded = sem("rows_loaded")
        w_loaded = sem("w_loaded")
        angle_loaded = [sem(f"angle{c}_loaded") for c in range(ANGLE_TILES)]
        ctxt_mm = sem("ctxt_mm")
        ctxt_ready = sem("ctxt_ready")
        kt_mm = sem("kt_mm")
        kthi_ready = sem("kthi_ready")
        ktlo_ready = sem("ktlo_ready")
        v_mm = sem("v_mm")
        v_ready = sem("v_ready")
        khi_stacked = sem("khi_stacked")
        kstack_loaded = sem("kstack_loaded")
        stack_filled = sem("stack_filled")
        whi_ready = sem("whi_ready")
        wlo_ready = sem("wlo_ready")
        angle_added = sem("angle_added")
        dve_angle_step = sem("dve_angle_step")
        pool_angle_step = sem("pool_angle_step")
        trig_ready = sem("trig_ready")
        trig_hi = sem("trig_hi")
        trig_lo = sem("trig_lo")
        x_loaded = [sem(f"x_loaded{b}") for b in range(NB)]
        out_stored = [sem(f"out_stored{b}") for b in range(NB)]
        bn_done = sem("bn_done")
        bn2_done = sem("bn2_done")
        stats1_ready = sem("stats1_ready")
        stats2_ready = sem("stats2_ready")
        vareps1_ready = sem("vareps1_ready")
        vareps2_ready = sem("vareps2_ready")
        rstd1_ready = sem("rstd1_ready")
        rstd2_ready = sem("rstd2_ready")
        xn1_ready = sem("xn1_ready")
        xn2_ready = sem("xn2_ready")
        xb_ready = sem("xb_ready")
        tr1_mm = sem("tr1_mm")
        xt1_hi = sem("xt1_hi")
        xt1_ready = sem("xt1_ready")
        q_mm = sem("q_mm")
        q_hi = sem("q_hi")
        q_ready = sem("q_ready")
        qstack_loaded = sem("qstack_loaded")
        kmask_ready = sem("kmask_ready")
        smax_mm = sem("smax_mm")
        max_ready = sem("max_ready")
        maxt_mm = sem("maxt_mm")
        negmax_ready = sem("negmax_ready")
        negmax_loaded = sem("negmax_loaded")
        st_mm = sem("st_mm")
        exp_done = sem("exp_done")
        pv_mm = sem("pv_mm")
        logden_done = sem("logden_done")
        rden_ready = sem("rden_ready")
        newton_a = sem("newton_a")
        newton_b = sem("newton_b")
        att_done = sem("att_done")
        att_hi = sem("att_hi")
        att_ready = sem("att_ready")
        wo_mm = sem("wo_mm")
        x2_ready = sem("x2_ready")
        tr2_mm = sem("tr2_mm")
        xt2_hi = sem("xt2_hi")
        xt2_ready = sem("xt2_ready")
        ffn_mm = sem("ffn_mm")
        sq_done = sem("sq_done")
        sum_ready = sem("sum_ready")
        root_ready = sem("root_ready")
        result_ready = sem("result_ready")

        x_tiles = x.rearrange("b (i p s) f -> b i p s f", p=P, s=SUB)
        out_tiles = out.rearrange("b (i p s) f -> b i p s f", p=P, s=SUB)

        def rows(w):
            return w.rearrange("(f p) n -> p f n", p=P)

        def smax_bank(i):
            bank = (scores, values_sums)[i % 4 // 2][:, i % 2]
            return bank.rearrange("p a t -> p (a t)")

        block = stack.enter_context(nc.Block())

        def angle_source(c):
            f = c % FT
            return (theta, theta_noise, wcos, f) if c < FT else (phi, phi_noise, wsin, f)

        def load_angle(eng, c):
            angle, noise, _, f = angle_source(c)
            if ANGLE_BUFFER[c] in ANGLE_BUFFER[:c]:
                last_there = max(i for i in range(c) if ANGLE_BUFFER[i] == ANGLE_BUFFER[c])
                eng.wait_ge(trig_lo, last_there + 1)
            for i, w in enumerate((angle, noise)):
                eng.dma_start(angle_in[c][:, i], w[P * f:P * (f + 1), :]).then_inc(angle_loaded[c], 16)

        def angle_offset(c):
            return PI / 2 if c < FT else 0.0

        @block.sync
        def _(sp):
            sp.dma_start(ctx_in, ctx_768.rearrange("b p c -> p b c")).then_inc(ctx_loaded, 16)
            sp.dma_start(wk_in, rows(w_k)).then_inc(wk_loaded, 16)
            sp.dma_start(xres[:, 0], x_tiles[0, 0]).then_inc(x_loaded[0], 16)
            load_angle(sp, 0)
            sp.dma_start(bk_col[:], b_k.rearrange("(f p) -> p f", p=P), allow_slow_non_contiguous=True).then_inc(bias_loaded, 16)
            sp.dma_start(bq_col[:], b_q.rearrange("(f p) -> p f", p=P), allow_slow_non_contiguous=True).then_inc(bias_loaded, 16)
            sp.wait_ge(ctxt_mm, CT)
            sp.dma_start(w_in, rows(w_q)).then_inc(w_loaded, 16)
            for c in range(CT):
                sp.dma_start(wv_in[c], w_v[P * c:P * (c + 1), :]).then_inc(wv_loaded, 16)
            load_angle(sp, 1)
            sp.dma_start(bv_row, b_v.partition_broadcast(P)).then_inc(rows_loaded, 16)
            sp.dma_start(bo_row[:], b_o.partition_broadcast(P)).then_inc(rows_loaded, 16)
            load_angle(sp, 2)
            load_angle(sp, 3)
            sp.wait_ge(wlo_ready, 1)
            sp.dma_start(w_in, rows(w_o)).then_inc(w_loaded, 16)
            load_angle(sp, 4)
            sp.wait_ge(kthi_ready, NG)
            sp.wait_ge(ktlo_ready, NG)
            for i, (part, loaded) in enumerate(((kt_hi, khi_stacked), (kt_hi, kstack_loaded), (kt_lo, kstack_loaded))):
                for j in range(HG):
                    sp.dma_start(kstack[HD * i:HD * (i + 1), j].bitcast(F32),
                                 part[HD * j:HD * (j + 1)].bitcast(F32)).then_inc(loaded, 16)

            def step(s):
                new, done, load = s + 1, s + -2, s + 2
                if is_step(done, NT - 1):
                    for w in range(SUB):
                        wait(sp, result_ready, done, SUB, w + 1)
                        sp.dma_start(out_tiles[done.batch, done.chunk][:, w],
                                     xres[:, done.batch, w]).then_inc(out_stored[done.batch], 16)
                elif done.exists:
                    wait(sp, result_ready, done, SUB, SUB)
                    sp.sem_inc(passed, 1)
                    sp.dma_start(out_tiles[done.batch, done.chunk], xres[:, done.batch]).then_inc(out_stored[done.batch], 16)
                if is_step(s, 0):
                    sp.wait_ge(v_mm, NB)
                    load_angle(sp, 7)

                def stack_q(i, part):
                    for j in range(HG):
                        sp.dma_start(qstack[HD * i:HD * (i + 1), j].bitcast(F32),
                                     qt[HD * j:HD * (j + 1), part].bitcast(F32)).then_inc(qstack_loaded, 16)

                if new.exists:
                    wait(sp, q_hi, new, 2, 2)
                    sp.sem_inc(passed, 1)
                    wait(sp, st_mm, s, PAIRS, PAIRS)
                    stack_q(0, 0)
                    stack_q(2, 0)
                if is_step(load, 1):
                    load_angle(sp, 5)
                if new.exists:
                    wait(sp, q_ready, new, 2, 2)
                    sp.sem_inc(passed, 1)
                    stack_q(1, 1)
                    if is_step(new, 0):
                        load_angle(sp, 6)
                    wait(sp, negmax_ready, new, 1, 1)
                    sp.dma_start(qstack[MAXROW:MAXROW + 1].rearrange("p j g t -> p (j g) t").bitcast(F32),
                                 negmax[:].bitcast(F32)).then_inc(negmax_loaded, 16)

            steps(sp, step)
            for b in range(NB):
                stores = NT // NB + (SUB - 1 if b == NB - 1 else 0)
                sp.wait_ge(out_stored[b], 16 * stores)

        @block.gpsimd
        def _(pool):
            pool.memset(ident[:], 0.0).then_inc(ident_zero, 1)
            pool.wait_ge(ident_zero, 1)
            pool.affine_select(out=ident[:], in_=ident[:], compare_op=ALU.not_equal, fill=1.0, base=0,
                               pattern=[[-1, P]], channel_multiplier=1).then_inc(consts_made, 1)
            pool.memset(ones[:], 1.0).then_inc(consts_made, 1)
            pool.memset(minus_half[:], -0.5).then_inc(consts_made, 1)
            pool.memset(eps[:], LN_EPS).then_inc(consts_made, 1)
            pool.memset(half_pi[:], PI / 2).then_inc(consts_made, 1)
            pool.wait_ge(consts_made, CONSTS)
            pool.memset(kstack[MAXROW:MAXROW + 1].bitcast(F32), 1.0).then_inc(stack_filled, 1)
            pool.wait_ge(stack_filled, 1)
            pool.memset(kmask[:].bitcast(F32), 0.0).then_inc(stack_filled, 1)

            def add_noise(c):
                pool.wait_ge(angle_loaded[c], 32)
                pool.tensor_tensor(angle_in[c][:, 0], angle_in[c][:, 0], angle_in[c][:, 1], ALU.add).then_inc(angle_added, 1)

            def reduce_angle(c, z):
                y, k = angle_in[c][:, 0], angle_in[c][:, 1]
                offset = angle_offset(c)
                n = POOL_ANGLE_STEPS * POOL_ANGLES.index(c)
                pool.wait_ge(angle_added, c + 1)
                pool.tensor_scalar(k, y, 1.0 / (2 * PI), offset / (2 * PI), ALU.mult, ALU.add).then_inc(pool_angle_step, 1)
                pool.wait_ge(pool_angle_step, n + 1)
                pool.tensor_scalar(k, k, 1.0, ROUND, ALU.mult, ALU.add).then_inc(pool_angle_step, 1)
                pool.wait_ge(pool_angle_step, n + 2)
                pool.tensor_scalar(k, k, 1.0, -ROUND, ALU.mult, ALU.add).then_inc(pool_angle_step, 1)
                for m, part in enumerate(TWO_PI_PARTS):
                    pool.wait_ge(pool_angle_step, n + 3 + 2 * m)
                    pool.tensor_scalar(z, k, -part, 0.0, ALU.mult, ALU.add).then_inc(pool_angle_step, 1)
                    pool.wait_ge(pool_angle_step, n + 4 + 2 * m)
                    pool.tensor_tensor(y, y, z, ALU.add).then_inc(pool_angle_step, 1)
                pool.wait_ge(pool_angle_step, n + 9)
                pool.tensor_scalar(y, y, -SIN_MAX - offset, SIN_MAX - offset, ALU.max, ALU.min).then_inc(pool_angle_step, 1)

            pool.wait_ge(stack_filled, STACK_CONSTS)

            def step(s):
                new, done = s + 2, s + -2

                def inverse_deviation(tile, part, stats_ready, vareps_ready, rstd_ready, xn_ready):
                    r = slice(SUB * part, SUB * (part + 1))
                    wait(pool, xn_ready, tile, 1, 0)
                    wait(pool, stats_ready, tile, 1, 1)
                    pool.tensor_tensor(vareps[:, r], meanvar[:, r, 1], eps[:, r], ALU.add).then_inc(vareps_ready, 1)
                    wait(pool, vareps_ready, tile, 1, 1)
                    pool.tensor_tensor(rstd[:, r], vareps[:, r], minus_half[:, r], ALU.pow).then_inc(rstd_ready, 1)

                if done.exists and not is_step(done, NT - 1):
                    wait(pool, root_ready, done, SUB, SUB)
                    for w in range(SUB):
                        pool.tensor_tensor(xres[:, done.batch, w], xres[:, done.batch, w], sq_real[:, w],
                                           ALU.add).then_inc(result_ready, 1)
                if is_step(s, FIRST):
                    add_noise(0)
                if new.exists:
                    inverse_deviation(new, 0, stats1_ready, vareps1_ready, rstd1_ready, xn1_ready)
                if is_step(s, FIRST + 1):
                    add_noise(5)
                if s.exists:
                    inverse_deviation(s, 1, stats2_ready, vareps2_ready, rstd2_ready, xn2_ready)
                if new.exists:
                    if is_step(s, FIRST):
                        add_noise(1)
                        pool.wait_ge(rows_loaded, 32)
                    wait(pool, xn1_ready, new, 1, 1)
                    for w in range(SUB):
                        last = pool.tensor_tensor(xres[:, new.batch, w], xres[:, new.batch, w], bo_row[:], ALU.add)
                    last.then_inc(xb_ready, 1)
                if is_step(s, FIRST):
                    add_noise(2)
                    add_noise(3)
                    add_noise(4)
                    reduce_angle(4, v_sb[:, NB - 1])
                if is_step(s, FIRST + 1):
                    pool.wait_ge(v_mm, NB)
                    for c in (6, 7):
                        add_noise(c)
                        reduce_angle(c, sq_imag)

            steps(pool, step)

        @block.scalar
        def _(act):
            for c in range(CT):
                act.wait_ge(ctxt_mm, c + 1)
                act.activation(ctx_t[c], gen[:, c, :], ACT.Copy).then_inc(ctxt_ready, 1)

            def trig(c):
                _, _, w, f = angle_source(c)
                y = angle_in[c][:, 0]
                if c in DVE_ANGLES:
                    act.wait_ge(dve_angle_step, DVE_ANGLE_STEPS * (DVE_ANGLES.index(c) + 1))
                else:
                    act.wait_ge(pool_angle_step, POOL_ANGLE_STEPS * (POOL_ANGLES.index(c) + 1))
                act.activation(y, y, ACT.Sin, bias=half_pi[:] if w is wcos else 0.0).then_inc(trig_ready, 1)
                act.wait_ge(trig_ready, c + 1)
                act.activation(w[:, 0, f], y, ACT.Copy).then_inc(trig_hi, 1)

            def weights_hi(w, n):
                act.wait_ge(w_loaded, 16 * n)
                act.activation(w[:, 0], w_in, ACT.Copy).then_inc(whi_ready, 1)

            def k_hi(g):
                act.wait_ge(kt_mm, g + 1)
                act.activation(kt_hi[:, g].rearrange("p b k -> p (b k)"), gen[:, g, :], ACT.Identity,
                               bias=bk_col[:, g:g + 1]).then_inc(kthi_ready, 1)

            act.wait_ge(consts_made, CONSTS)
            act.wait_ge(bias_loaded, 32)
            k_hi(0)
            trig(0)
            k_hi(1)
            weights_hi(wq, 1)
            k_hi(2)
            trig(1)
            k_hi(3)

            def step(s):
                q_tile, t1, ffn, done = s + 1, s + 2, s + -1, s + -2

                def exps(tile, k):
                    wait(act, st_mm, tile, PAIRS, k + 1)
                    wait(act, pv_mm, tile, NG, k // 2 - 1)
                    act.activation(probs[:, k % 4], scores[:, k % 2], ACT.Exp, scale=SCALE).then_inc(exp_done, 1)

                def log_sums(g):
                    wait(act, pv_mm, s, NG, g + 1)
                    wait(act, att_done, s, NG, g - 1)
                    act.activation(rden[:, g % 2], values_sums[:, g % 2, 1], ACT.Ln).then_inc(logden_done, 1)

                def inverse_sums(g):
                    wait(act, logden_done, s, NG, g + 1)
                    act.activation(rden[:, g % 2], rden[:, g % 2], ACT.Exp, scale=-1.0).then_inc(rden_ready, 1)

                def square(u):
                    wait(act, ffn_mm, ffn, 2 * SUB, u + 1)
                    if u == 0:
                        wait(act, result_ready, ffn, SUB, 0)
                    if u % 2:
                        wait(act, sum_ready, ffn, SUB, u // 2)
                    act.activation(sq_imag if u % 2 else sq_real[:, u // 2], gen[:, FFN_BANK[u], :],
                                   ACT.Square).then_inc(sq_done, 1)

                def last_roots(w):
                    wait(act, sum_ready, ffn, SUB, w + 1)
                    act.activation(sq_real[:, w], sq_real[:, w], ACT.Sqrt).then_inc(root_ready, 1)

                def transposed_hi(tile, xt, banks, done, ready, parts=(0, 1)):
                    for k in parts:
                        wait(act, done, tile, 2, k + 1)
                        act.activation(xt[:, 0, 2 * k:2 * k + 2].rearrange("p f t -> p (f t)"), gen[:, banks[k], :],
                                       ACT.Copy).then_inc(ready, 1)

                def last_x2_part():
                    if ffn.exists:
                        transposed_hi(ffn, xt2, TR2_BANK, tr2_mm, xt2_hi, (1,))

                def load_x():
                    if done.exists:
                        act.wait_ge(out_stored[done.batch], 16 * (done.chunk + 1))
                        act.sem_inc(passed, 1)
                    act.dma_start(xres[:, t1.batch], x_tiles[t1.batch, t1.chunk]).then_inc(x_loaded[t1.batch], 16)

                if is_step(t1, 1):
                    act.wait_ge(trig_lo, 3)
                    load_x()
                if is_step(t1, 2):
                    act.wait_ge(v_mm, NB)
                    load_x()
                if is_step(s, 0):
                    act.wait_ge(wlo_ready, 2)
                if s.exists:
                    for k in range(2 if starts_early(s) else 0, 4):
                        exps(s, k)
                    for g in range(NG):
                        log_sums(g)
                        inverse_sums(g)
                        if g == 1:
                            last_x2_part()
                        if g + 2 < NG:
                            exps(s, 2 * g + 4)
                            exps(s, 2 * g + 5)
                else:
                    last_x2_part()
                if done.exists and not is_step(done, NT - 1):
                    wait(act, sum_ready, done, SUB, SUB)
                    act.activation(sq_real, sq_real, ACT.Sqrt).then_inc(root_ready, SUB)
                    if q_tile.exists:
                        act.preload_act_table_set(EXP_LN_SET)
                if q_tile.exists:
                    wait(act, qstack_loaded, s, 16 * 3 * HG, 16 * 3 * HG)
                    wait(act, smax_mm, s, SUB * NG, SUB * NG)
                    for k in range(2):
                        wait(act, q_mm, q_tile, 2, k + 1)
                        for i in range(2):
                            g = 2 * k + i
                            last = act.activation(qt[:, 0, g], gen[:, Q_BANK[k], T * i:T * (i + 1)], ACT.Identity,
                                                  bias=bq_col[:, g:g + 1])
                        last.then_inc(q_hi, 1)
                if is_step(s, FIRST + 1):
                    weights_hi(wo, 2)
                    trig(3)
                    trig(4)
                if is_step(s, 0):
                    trig(5)
                    trig(6)
                    trig(7)
                    act.preload_act_table_set(EXP_LN_SET)
                if t1.exists and not loaded_early(t1):
                    load_x()
                if is_step(s, 1):
                    act.wait_ge(trig_lo, ANGLE_TILES)
                if ffn.exists:
                    square(0)
                if q_tile.exists:
                    wait(act, maxt_mm, q_tile, 1, 1)
                    wait(act, negmax_loaded, s, 16, 16)
                    act.activation(negmax[:], gen[0:NH, MAXT_BANK, 0:T], ACT.Copy, scale=-1.0).then_inc(negmax_ready, 1)
                if ffn.exists:
                    square(1)
                if is_step(s, FIRST):
                    transposed_hi(t1, xt1, TR1_BANK, tr1_mm, xt1_hi)
                    trig(2)
                    act.wait_ge(stack_filled, STACK_CONSTS)
                    act.wait_ge(khi_stacked, 16 * HG)
                if t1.exists:
                    wait(act, smax_mm, q_tile, SUB * NG, SUB * NG)
                    for j in range(HG):
                        last = act.activation(kmask[HD * j:HD * (j + 1), :, j, :],
                                              kstack[0:HD, j, :, t1.batch, :].bitcast(F32), ACT.Copy)
                    last.then_inc(kmask_ready, 1)
                if ffn.exists:
                    square(2)

                if t1.exists and not is_step(s, FIRST):
                    wait(act, q_mm, q_tile, 2, 2)
                    transposed_hi(t1, xt1, TR1_BANK, tr1_mm, xt1_hi)
                if q_tile.exists and starts_early(q_tile):
                    exps(q_tile, 0)
                    exps(q_tile, 1)
                if is_step(ffn, NT - 1):
                    last_roots(0)
                if ffn.exists:
                    square(3)
                if is_step(ffn, NT - 1):
                    last_roots(1)
                if s.exists:
                    wait(act, ffn_mm, ffn, 2 * SUB, 2 * SUB)
                    transposed_hi(s, xt2, TR2_BANK, tr2_mm, xt2_hi, (0,))
                if is_step(s, FIRST + 1):
                    act.preload_act_table_set(EXP_LN_SET)

            steps(act, step)

        @block.vector
        def _(dve):
            def reduce_angle(c):
                y, k = angle_in[c][:, 0], angle_in[c][:, 1]
                offset = angle_offset(c)
                n = DVE_ANGLE_STEPS * DVE_ANGLES.index(c)
                dve.wait_ge(angle_added, c + 1)
                dve.tensor_scalar(k, y, 1.0 / (2 * PI), offset / (2 * PI), ALU.mult, ALU.add).then_inc(dve_angle_step, 1)
                dve.wait_ge(dve_angle_step, n + 1)
                dve.tensor_scalar(k, k, ROUND, ROUND, ALU.add, ALU.subtract).then_inc(dve_angle_step, 1)
                for m, part in enumerate(TWO_PI_PARTS):
                    dve.wait_ge(dve_angle_step, n + 2 + m)
                    dve.scalar_tensor_tensor(y, k, -part, y, ALU.mult, ALU.add).then_inc(dve_angle_step, 1)
                dve.wait_ge(dve_angle_step, n + 5)
                dve.tensor_scalar(y, y, -SIN_MAX - offset, SIN_MAX - offset, ALU.max, ALU.min).then_inc(dve_angle_step, 1)

            def weights_lo(w, n):
                dve.wait_ge(whi_ready, n)
                dve.tensor_tensor(w[:, 1], w_in, w[:, 0].bitcast(F32), ALU.subtract).then_inc(wlo_ready, 1)

            def trig_rest(c):
                _, _, w, f = angle_source(c)
                dve.wait_ge(trig_hi, c + 1)
                dve.tensor_tensor(w[:, 1, f], angle_in[c][:, 0], w[:, 0, f].bitcast(F32),
                                  ALU.subtract).then_inc(trig_lo, 1)

            def values_in(b):
                dve.wait_ge(v_mm, b + 1)
                dve.tensor_tensor(v_sb[:, b], gen[:, V_BANK[b], :], bv_row, ALU.add).then_inc(v_ready, 1)

            def k_lo(g):
                dve.wait_ge(kthi_ready, g + 1)
                dve.scalar_tensor_tensor(kt_lo[:, g].rearrange("p b k -> p (b k)"), gen[:, g, :], bk_col[:, g:g + 1],
                                         kt_hi[:, g].rearrange("p b k -> p (b k)").bitcast(F32),
                                         ALU.add, ALU.subtract).then_inc(ktlo_ready, 1)

            def step(s):
                q_tile, t1, ffn = s + 1, s + 2, s + -1

                def normalise(tile, part, transposed, rstd_ready, ready):
                    wait(dve, rstd_ready, tile, 1, 1)
                    wait(dve, transposed, tile, 2, 0)
                    for w in range(SUB):
                        r = SUB * part + w
                        last = dve.tensor_scalar(xn[:, part, w], xres[:, tile.batch, w], meanvar[:, r, 0:1],
                                                 rstd[:, r:r + 1], ALU.subtract, ALU.mult)
                    last.then_inc(ready, 1)

                def row_stats(tile, part, w, ready, done):
                    wait(dve, ready, tile, SUB, w + 1)
                    dve.bn_stats(stats[:, SUB * part + w], xres[:, tile.batch, w]).then_inc(done, 1)

                def aggregate(tile, part, done, ready):
                    wait(dve, done, tile, SUB, SUB)
                    dve.sem_inc(passed, 1)
                    for w in range(SUB):
                        last = dve.bn_aggr(meanvar[:, SUB * part + w], stats[:, SUB * part + w])
                    last.then_inc(ready, 1)

                def x_stats():
                    dve.wait_ge(x_loaded[t1.batch], 16 * (t1.chunk + 1))
                    for w in range(SUB):
                        dve.bn_stats(stats[:, w], xres[:, t1.batch, w]).then_inc(bn_done, 1)
                    aggregate(t1, 0, bn_done, stats1_ready)

                def residual(w):
                    wait(dve, wo_mm, s, SUB, w + 1)
                    dve.tensor_tensor(xres[:, s.batch, w], gen[:, WO_BANK[w], :], xres[:, s.batch, w],
                                      ALU.add).then_inc(x2_ready, 1)

                def maxima(some):
                    for i in some:
                        w, g = i // NG, i % NG
                        wait(dve, smax_mm, q_tile, SUB * NG, i + 1)
                        dve.tensor_reduce(rowmax[:, w].rearrange("p (j g) -> p g j", g=NG)[:, g],
                                          smax_bank(i).rearrange("p (j k) -> p j k", j=HG),
                                          AX.X, ALU.max).then_inc(max_ready, 1)

                def add_squares(w):
                    wait(dve, sq_done, ffn, 2 * SUB, 2 * w + 2)
                    dve.tensor_tensor(sq_real[:, w], sq_real[:, w], sq_imag, ALU.add).then_inc(sum_ready, 1)

                def last_result(w):
                    wait(dve, root_ready, ffn, SUB, w + 1)
                    dve.tensor_tensor(xres[:, ffn.batch, w], xres[:, ffn.batch, w], sq_real[:, w],
                                      ALU.add).then_inc(result_ready, 1)

                def transposed_lo(tile, xt, banks, hi_done, ready, parts=(0, 1)):
                    for k in parts:
                        wait(dve, hi_done, tile, 2, k + 1)
                        dve.tensor_tensor(xt[:, 1, 2 * k:2 * k + 2].rearrange("p f t -> p (f t)"), gen[:, banks[k], :],
                                          xt[:, 0, 2 * k:2 * k + 2].rearrange("p f t -> p (f t)").bitcast(F32),
                                          ALU.subtract).then_inc(ready, 1)

                if s.exists:
                    wait(dve, wo_mm, s, SUB, 0)

                    def att_hi_part(g):
                        wait(dve, att_done, s, NG, g + 1)
                        dve.tensor_copy(att_t[:, 0, g], att[:, g % 2]).then_inc(att_hi, 1)

                    def att_lo_part(g):
                        wait(dve, att_hi, s, NG, g + 1)
                        dve.tensor_tensor(att_t[:, 1, g], att[:, g % 2], att_t[:, 0, g].bitcast(F32),
                                          ALU.subtract).then_inc(att_ready, 1)

                    for g in range(NG):
                        r, a = rden[:, g % 2], att[:, g % 2]
                        wait(dve, rden_ready, s, NG, g + 1)
                        wait(dve, att_ready, s, NG, g - 1)
                        dve.tensor_tensor(a, values_sums[:, g % 2, 1], r, ALU.mult).then_inc(newton_a, 1)
                        if g > 0:
                            att_hi_part(g - 1)
                        wait(dve, newton_a, s, NG, g + 1)
                        dve.scalar_tensor_tensor(r, a, 2.0, r, ALU.subtract, ALU.mult).then_inc(newton_b, 1)
                        if g > 0:
                            att_lo_part(g - 1)
                        wait(dve, newton_b, s, NG, g + 1)
                        dve.scalar_tensor_tensor(a, values_sums[:, g % 2, 0], -1.0, r, ALU.mult, ALU.mult).then_inc(att_done, 1)
                        if g == 1 and ffn.exists:
                            transposed_lo(ffn, xt2, TR2_BANK, xt2_hi, xt2_ready, (1,))
                    att_hi_part(NG - 1)
                    att_lo_part(NG - 1)
                elif ffn.exists:
                    transposed_lo(ffn, xt2, TR2_BANK, xt2_hi, xt2_ready, (1,))
                if is_step(s, FIRST + 1):
                    dve.wait_ge(rows_loaded, 32)
                    values_in(0)
                if q_tile.exists:
                    for k in range(2):
                        wait(dve, q_hi, q_tile, 2, k + 1)
                        for i in range(2):
                            g = 2 * k + i
                            last = dve.scalar_tensor_tensor(qt[:, 1, g], gen[:, Q_BANK[k], T * i:T * (i + 1)],
                                                            bq_col[:, g:g + 1], qt[:, 0, g].bitcast(F32),
                                                            ALU.add, ALU.subtract)
                        last.then_inc(q_ready, 1)
                if is_step(t1, 2):
                    x_stats()
                if s.exists:
                    wait(dve, xb_ready, s, 1, 1)
                    residual(0)
                    row_stats(s, 1, 0, x2_ready, bn2_done)
                if q_tile.exists:
                    wait(dve, maxt_mm, s, 1, 1)
                    if is_step(s, FIRST + 1):
                        values_in(1)
                    maxima(range(2))
                if s.exists:
                    residual(1)
                if q_tile.exists:
                    maxima(range(2, 4))
                    if is_step(s, FIRST + 1):
                        trig_rest(3)
                        x_stats()
                        values_in(2)
                if s.exists:
                    row_stats(s, 1, 1, x2_ready, bn2_done)
                if q_tile.exists:
                    maxima(range(4, SUB * NG))
                    if is_step(s, FIRST + 1):
                        trig_rest(4)
                        values_in(3)
                if t1.exists and (is_step(t1, 0) or not loaded_early(t1)):
                    x_stats()
                if is_step(s, 0):
                    trig_rest(5)
                    trig_rest(6)
                    trig_rest(7)
                if is_step(s, FIRST):
                    reduce_angle(0)
                    dve.wait_ge(bias_loaded, 32)
                if t1.exists:
                    normalise(t1, 0, tr1_mm, rstd1_ready, xn1_ready)
                if s.exists:
                    aggregate(s, 1, bn2_done, stats2_ready)
                if ffn.exists:
                    add_squares(0)
                if is_step(s, FIRST):
                    k_lo(0)
                    trig_rest(0)
                    k_lo(1)
                    reduce_angle(1)
                    weights_lo(wq, 1)
                    k_lo(2)
                    trig_rest(1)
                    k_lo(3)
                if is_step(s, FIRST + 1):
                    weights_lo(wo, 2)
                if t1.exists:
                    transposed_lo(t1, xt1, TR1_BANK, xt1_hi, xt1_ready)
                if s.exists:
                    normalise(s, 1, tr2_mm, rstd2_ready, xn2_ready)
                if is_step(ffn, NT - 1):
                    last_result(0)
                if ffn.exists:
                    add_squares(1)
                if is_step(ffn, NT - 1):
                    last_result(1)
                if s.exists:
                    transposed_lo(s, xt2, TR2_BANK, xt2_hi, xt2_ready, (0,))
                if is_step(s, FIRST):
                    reduce_angle(2)
                    trig_rest(2)
                    reduce_angle(3)
                if is_step(s, FIRST + 1):
                    reduce_angle(5)

            steps(dve, step)

        @block.tensor
        def _(pe):
            def product3(out_, left, right, k_tiles=range(FT)):
                for f in k_tiles:
                    for n, (a, b) in enumerate(((0, 0), (0, 1), (1, 0))):
                        last = pe.matmul(out_, left(a, f), right(b, f), start=(f == 0 and n == 0),
                                         stop=(f == FT - 1 and n == 2))
                return last

            pe.wait_ge(consts_made, CONSTS)
            pe.wait_ge(ctx_loaded, 16)
            for c in range(CT):
                for b in range(NB):
                    last = pe.transpose(gen[:, c, LK * b:LK * (b + 1)], ctx_in[:, b, P * c:P * (c + 1)], ident[:])
                last.then_inc(ctxt_mm, 1)
            pe.wait_ge(ctxt_ready, CT)
            pe.wait_ge(wk_loaded, 16)
            for g in range(NG):
                for c in range(CT):
                    last = pe.matmul(gen[:, g, :], wk_in[:, c, P * g:P * (g + 1)], ctx_t[c],
                                     start=(c == 0), stop=(c == CT - 1))
                last.then_inc(kt_mm, 1)

            def v_product(b):
                if b == 0:
                    pe.wait_ge(wv_loaded, 16 * CT)
                    pe.wait_ge(ktlo_ready, NG)
                if b >= 2:
                    pe.wait_ge(v_ready, b - 1)
                for c in range(CT):
                    last = pe.matmul(gen[:, V_BANK[b], :], ctx_t[c][:, LK * b:LK * (b + 1)], wv_in[c],
                                     start=(c == 0), stop=(c == CT - 1))
                last.then_inc(v_mm, 1)

            def step(s):
                q_tile, t1, ffn = s + 1, s + 2, s + -1

                def pair_scores(tile, k):
                    g, j0 = k // 2, 2 * (k % 2)
                    if k == 0:
                        wait(pe, qstack_loaded, tile, 16 * 3 * HG, 16 * 3 * HG)
                        wait(pe, negmax_loaded, tile, 16, 16)
                    wait(pe, exp_done, tile, PAIRS, k - 1)
                    for i in range(2):
                        last = pe.matmul(scores[:, k % 2, i], kstack[0:KROWS, j0 + i, g, tile.batch],
                                         qstack[0:KROWS, j0 + i, g], start=True, stop=True)
                    last.then_inc(st_mm, 1)

                def values(g):
                    wait(pe, exp_done, s, PAIRS, 2 * g + 2)
                    wait(pe, att_done, s, NG, g - 1)
                    for part in range(2):
                        for j in range(HG):
                            h = HG * g + j
                            last = pe.matmul(values_sums[HD * j:HD * (j + 1), g % 2, part],
                                             ones[:] if part else v_sb[:, s.batch, HD * h:HD * (h + 1)],
                                             probs[:, (2 * g + j // 2) % 4, j % 2], start=True, stop=True,
                                             tile_position=(0, HD * j))
                    last.then_inc(pv_mm, 1)

                def q_group(g):
                    if not q_tile.exists:
                        return
                    if g == 0:
                        if is_step(q_tile, 0):
                            pe.wait_ge(wlo_ready, 1)
                        wait(pe, xt1_ready, q_tile, 2, 2)
                        wait(pe, xt2_ready, ffn, 2, 1)
                    last = product3(gen[:, Q_BANK[g // 2], T * (g % 2):T * (g % 2 + 1)],
                                    lambda a, f: wq[:, a, f, P * g:P * (g + 1)],
                                    lambda b, f: xt1[:, b, f])
                    if g % 2:
                        last.then_inc(q_mm, 1)

                if is_step(s, 0):
                    pe.wait_ge(kstack_loaded, 16 * 2 * HG)
                    pe.wait_ge(v_ready, NB)
                if s.exists:
                    if not starts_early(s):
                        pair_scores(s, 0)
                        pair_scores(s, 1)
                    for g in range(NG):
                        if g == 2:
                            q_group(0)
                        if g + 1 < NG:
                            pair_scores(s, 2 * g + 2)
                            pair_scores(s, 2 * g + 3)
                        values(g)
                else:
                    if is_step(s, FIRST + 1):
                        v_product(0)
                    q_group(0)
                for g in range(1, NG):
                    q_group(g)
                if is_step(s, FIRST + 1):
                    v_product(1)
                def scores_for_max(some):
                    for i in some:
                        w, g = i // NG, i % NG
                        if i >= 4:
                            wait(pe, max_ready, q_tile, SUB * NG, i - 3)
                        pe.matmul(smax_bank(i), qt[:, 0, g, P * w:P * (w + 1)],
                                  kmask[:, g].rearrange("p j k -> p (j k)"), start=True, stop=True).then_inc(smax_mm, 1)

                def feed_forward(u, k_tiles=range(FT)):
                    w, weights = u // 2, wsin if u % 2 else wcos
                    if is_step(ffn, 0) and u < 2:
                        pe.wait_ge(trig_lo, FT * (u + 1))
                    last = product3(gen[:, FFN_BANK[u], :], lambda a, f: xt2[:, a, f, P * w:P * (w + 1)],
                                    lambda b, f: weights[:, b, f], k_tiles)
                    if FT - 1 in k_tiles:
                        last.then_inc(ffn_mm, 1)

                def transposes(part, banks, done):
                    for k in range(2):
                        for f in (2 * k, 2 * k + 1):
                            for w in range(SUB):
                                at = T * (f % 2) + P * w
                                last = pe.transpose(gen[:, banks[k], at:at + P], xn[:, part, w, P * f:P * (f + 1)], ident[:])
                        last.then_inc(done, 1)

                def output_projection(w):
                    product3(gen[:, WO_BANK[w], :], lambda a, f: att_t[:, a, f, P * w:P * (w + 1)],
                             lambda b, f: wo[:, b, f]).then_inc(wo_mm, 1)

                if ffn.exists and not q_tile.exists:
                    wait(pe, xt2_ready, ffn, 2, 2)
                    wait(pe, sq_done, s + -2, 2 * SUB, 2 * SUB)
                    feed_forward(0)
                    feed_forward(1)
                if s.exists:
                    if is_step(s, 0):
                        pe.wait_ge(wlo_ready, 2)
                    wait(pe, att_ready, s, NG, NG)
                    wait(pe, sq_done, s + -2, 2 * SUB, 2 * SUB)
                    wait(pe, xt2_ready, ffn, 2, 2)
                    output_projection(0)
                if q_tile.exists:
                    wait(pe, kmask_ready, q_tile, 1, 1)
                    wait(pe, q_hi, q_tile, 2, 2)
                    wait(pe, att_done, s, NG, NG)
                    wait(pe, exp_done, s, PAIRS, PAIRS)
                    scores_for_max(range(4))
                if s.exists:
                    output_projection(1)
                if is_step(s, FIRST + 1):
                    v_product(2)
                if q_tile.exists:
                    scores_for_max(range(4, 6))
                    wait(pe, q_ready, q_tile, 2, 2)
                if ffn.exists and q_tile.exists:
                    wait(pe, xt2_ready, ffn, 2, 2)
                    feed_forward(0)
                if q_tile.exists:
                    scores_for_max(range(6, SUB * NG))
                if is_step(s, FIRST + 1):
                    v_product(3)
                    pe.wait_ge(v_ready, 3)
                if ffn.exists and q_tile.exists:
                    feed_forward(1, range(FT - 1))
                if q_tile.exists:
                    wait(pe, max_ready, q_tile, SUB * NG, SUB * NG)
                    wait(pe, x2_ready, s, SUB, 1)
                    for w in range(SUB):
                        last = pe.transpose(gen[0:NH, MAXT_BANK, P * w:P * (w + 1)], rowmax[:, w], ident[:])
                    last.then_inc(maxt_mm, 1)
                if ffn.exists and q_tile.exists:
                    feed_forward(1, range(FT - 1, FT))
                if ffn.exists:
                    wait(pe, x2_ready, s, SUB, SUB)
                    feed_forward(2)
                if is_step(s, FIRST):
                    pe.wait_ge(ktlo_ready, 2)
                if t1.exists:
                    wait(pe, xn1_ready, t1, 1, 1)
                    wait(pe, sq_done, ffn, 2 * SUB, 2)
                    transposes(0, TR1_BANK, tr1_mm)
                if q_tile.exists and starts_early(q_tile):
                    pair_scores(q_tile, 0)
                    pair_scores(q_tile, 1)
                if ffn.exists:
                    wait(pe, negmax_ready, q_tile, 1, 1)
                    wait(pe, sq_done, s + -2, 2 * SUB, 2 * SUB)
                    feed_forward(3)
                if s.exists:
                    wait(pe, xn2_ready, s, 1, 1)
                    wait(pe, sq_done, ffn, 2 * SUB, 3)
                    if t1.exists:
                        wait(pe, xt1_ready, t1, 2, 1)
                    transposes(1, TR2_BANK, tr2_mm)

            steps(pe, step)


_INS = ["x", "ctx_768", "L0_xattn_w_q", "L0_xattn_b_q", "L0_xattn_w_k", "L0_xattn_b_k", "L0_xattn_w_v",
        "L0_xattn_b_v", "L0_xattn_w_o", "L0_xattn_b_o", "L0_ffn_theta", "L0_ffn_phi",
        "L0_ffn_theta_noise", "L0_ffn_phi_noise"]


def kernel(**inputs):
    import numpy as _np
    import concourse.bacc as _bacc
    from concourse import mybir as _mybir
    from concourse.bass_utils import run_bass_kernel_spmd as _run

    nc = _bacc.Bacc("TRN2", target_bir_lowering=False, num_devices=1)
    arrays, args = {}, []
    for name in _INS:
        a = _np.ascontiguousarray(inputs[name])
        arrays[f"in_{name}_dram"] = a
        args.append(nc.dram_tensor(f"in_{name}_dram", a.shape, _mybir.dt.from_np(a.dtype), kind="ExternalInput").ap())
    shape = _np.shape(inputs["x"])
    args.append(nc.dram_tensor("out_0_dram", shape, _mybir.dt.float32, kind="ExternalOutput").ap())
    xattn_ffn(nc, *args)
    r = _run(nc, [arrays], core_ids=[0])
    return r.results[0]["out_0_dram"]
```
